# Optimizing a Trainium2 kernel written in Bass

```python
import numpy as np
import jax
import jax.numpy as jnp

def _softmax(x, axis=-1):
    return jax.nn.softmax(x, axis=axis)

def _gelu(x):
    return jax.nn.gelu(x, approximate=True)

def _silu(x):
    return jax.nn.silu(x)

def _sigmoid(x):
    return jax.nn.sigmoid(x)

def _layernorm(x, axis=-1, eps=1e-05):
    m = jnp.mean(x, axis=axis, keepdims=True)
    v = jnp.var(x, axis=axis, keepdims=True)
    return (x - m) / jnp.sqrt(v + eps)

def _scatter_add(tgt, idx, src, axis=0):
    return tgt.at[idx].add(src)

def _segment_sum(src, seg, n):
    return jax.ops.segment_sum(src, seg, n)
kernel_name = 'mk_macaron_d1_jaxref_r8_ae9dce'

def setup_inputs(seed: int=0):
    np.random.seed(seed)
    _w = jnp.asarray

    def _L0_attn_setup():
        import jax, jax.numpy as jnp
        import numpy as np
        B, T, C = (4, 512, 128)
        NUM_LAYERS = 24
        LAYER_ID = 0
        EPS = 1e-05

        def _ln(x, w, b):
            m = x.mean(-1, keepdims=True)
            v = x.var(-1, keepdims=True)
            return (x - m) / jnp.sqrt(v + EPS) * w + b

        def _time_shift(x):
            return jnp.pad(x, ((0, 0), (1, 0), (0, 0)))[:, :-1]

        def _wkv(w, u, k, v):

            def step(carry, kv_t):
                aa, bb, pp = carry
                kt, vt = kv_t
                ww = u + kt
                p = jnp.maximum(pp, ww)
                e1 = jnp.exp(pp - p)
                e2 = jnp.exp(ww - p)
                y = (e1 * aa + e2 * vt) / (e1 * bb + e2)
                ww2 = pp + w
                p2 = jnp.maximum(ww2, kt)
                e1 = jnp.exp(ww2 - p2)
                e2 = jnp.exp(kt - p2)
                return ((e1 * aa + e2 * vt, e1 * bb + e2, p2), y)
            Bz, Tz, Cz = k.shape
            init = (jnp.zeros((Bz, Cz), k.dtype), jnp.zeros((Bz, Cz), k.dtype), jnp.full((Bz, Cz), -1e+38, k.dtype))
            kT = jnp.swapaxes(k, 0, 1)
            vT = jnp.swapaxes(v, 0, 1)
            _, y = jax.lax.scan(step, init, (kT, vT))
            return jnp.swapaxes(y, 0, 1)
        key = jax.random.key(seed)
        ks = jax.random.split(key, 9)
        s = 0.02
        ratio_0_to_1 = LAYER_ID / (NUM_LAYERS - 1)
        ratio_1_to_almost0 = 1.0 - LAYER_ID / NUM_LAYERS
        h = np.arange(C, dtype=np.float64)
        time_decay = (-5.0 + 8.0 * (h / (C - 1)) ** (0.7 + 1.3 * ratio_0_to_1)).astype(np.float32)
        zigzag = ((np.arange(C) + 1) % 3 - 1) * 0.5
        time_first = (np.ones(C) * np.log(0.3) + zigzag).astype(np.float32)
        xi = np.arange(C, dtype=np.float64) / C
        tmk = (xi ** ratio_1_to_almost0).astype(np.float32)
        tmv = (xi ** ratio_1_to_almost0 + 0.3 * ratio_0_to_1).astype(np.float32)
        tmr = (xi ** (0.5 * ratio_1_to_almost0)).astype(np.float32)
        cmk = (xi ** ratio_1_to_almost0).astype(np.float32)
        H = 4 * C
        return {'x': jax.random.normal(ks[0], (B, T, C), jnp.float32), 'ln0_w': jnp.ones(C), 'ln0_b': jnp.zeros(C), 'ln1_w': jnp.ones(C), 'ln1_b': jnp.zeros(C), 'ln2_w': jnp.ones(C), 'ln2_b': jnp.zeros(C), 'time_decay': jnp.asarray(time_decay), 'time_first': jnp.asarray(time_first), 'tmk': jnp.asarray(tmk), 'tmv': jnp.asarray(tmv), 'tmr': jnp.asarray(tmr), 'Wk': jax.random.normal(ks[1], (C, C), jnp.float32) * s, 'Wv': jax.random.normal(ks[2], (C, C), jnp.float32) * s, 'Wr': jax.random.normal(ks[3], (C, C), jnp.float32) * s, 'Wo': jax.random.normal(ks[4], (C, C), jnp.float32) * s, 'cmk': jnp.asarray(cmk), 'cmr': jnp.asarray(cmk), 'Wfk': jax.random.normal(ks[5], (H, C), jnp.float32) * s, 'Wfr': jax.random.normal(ks[6], (C, C), jnp.float32) * s, 'Wfv': jax.random.normal(ks[7], (C, H), jnp.float32) * s}
    _L0_attn_in = _L0_attn_setup()

    def _L0_ffn_setup():
        import jax, jax.numpy as jnp
        import numpy as np
        B, S, D = (4, 256, 128)
        O = 128
        E = 8
        K = 2
        key = jax.random.key(seed)
        k1, k2, k3, k4, k5 = jax.random.split(key, 5)
        scale = 1.0 / np.sqrt(D)
        x = jax.random.normal(k1, (B, S, D), dtype=jnp.float32)
        We = jax.random.uniform(k2, (E, D, O), dtype=jnp.float32, minval=-scale, maxval=scale)
        be = jax.random.uniform(k3, (E, O), dtype=jnp.float32, minval=-scale, maxval=scale)
        Wg = jax.random.uniform(k4, (D, E), dtype=jnp.float32, minval=-scale, maxval=scale)
        bg = jax.random.uniform(k5, (E,), dtype=jnp.float32, minval=-scale, maxval=scale)
        return {'x': x, 'We': We, 'be': be, 'Wg': Wg, 'bg': bg}
    _L0_ffn_in = _L0_ffn_setup()
    _d = {'L0_attn_x': _L0_attn_in['x'], 'L0_attn_ln0_w': _L0_attn_in['ln0_w'], 'L0_attn_ln0_b': _L0_attn_in['ln0_b'], 'L0_attn_ln1_w': _L0_attn_in['ln1_w'], 'L0_attn_ln1_b': _L0_attn_in['ln1_b'], 'L0_attn_ln2_w': _L0_attn_in['ln2_w'], 'L0_attn_ln2_b': _L0_attn_in['ln2_b'], 'L0_attn_time_decay': _L0_attn_in['time_decay'], 'L0_attn_time_first': _L0_attn_in['time_first'], 'L0_attn_tmk': _L0_attn_in['tmk'], 'L0_attn_tmv': _L0_attn_in['tmv'], 'L0_attn_tmr': _L0_attn_in['tmr'], 'L0_attn_Wk': _L0_attn_in['Wk'], 'L0_attn_Wv': _L0_attn_in['Wv'], 'L0_attn_Wr': _L0_attn_in['Wr'], 'L0_attn_Wo': _L0_attn_in['Wo'], 'L0_attn_cmk': _L0_attn_in['cmk'], 'L0_attn_cmr': _L0_attn_in['cmr'], 'L0_attn_Wfk': _L0_attn_in['Wfk'], 'L0_attn_Wfr': _L0_attn_in['Wfr'], 'L0_attn_Wfv': _L0_attn_in['Wfv'], 'L0_ffn_We': _L0_ffn_in['We'], 'L0_ffn_be': _L0_ffn_in['be'], 'L0_ffn_Wg': _L0_ffn_in['Wg'], 'L0_ffn_bg': _L0_ffn_in['bg']}
    _x0 = _d['L0_attn_x']
    _d['L0_attn_x'] = jax.random.normal(jax.random.fold_in(jax.random.key(seed), 1), (4, 512, 128), dtype=_x0.dtype)
    del _x0
    return _d

def reference(L0_attn_x, L0_attn_ln0_w, L0_attn_ln0_b, L0_attn_ln1_w, L0_attn_ln1_b, L0_attn_ln2_w, L0_attn_ln2_b, L0_attn_time_decay, L0_attn_time_first, L0_attn_tmk, L0_attn_tmv, L0_attn_tmr, L0_attn_Wk, L0_attn_Wv, L0_attn_Wr, L0_attn_Wo, L0_attn_cmk, L0_attn_cmr, L0_attn_Wfk, L0_attn_Wfr, L0_attn_Wfv, L0_ffn_We, L0_ffn_be, L0_ffn_Wg, L0_ffn_bg):

    def _L0_attn_ref(x, ln0_w, ln0_b, ln1_w, ln1_b, ln2_w, ln2_b, time_decay, time_first, tmk, tmv, tmr, Wk, Wv, Wr, Wo, cmk, cmr, Wfk, Wfr, Wfv):
        import jax, jax.numpy as jnp
        import numpy as np
        B, T, C = (4, 512, 128)
        NUM_LAYERS = 24
        LAYER_ID = 0
        EPS = 1e-05

        def _ln(x, w, b):
            m = x.mean(-1, keepdims=True)
            v = x.var(-1, keepdims=True)
            return (x - m) / jnp.sqrt(v + EPS) * w + b

        def _time_shift(x):
            return jnp.pad(x, ((0, 0), (1, 0), (0, 0)))[:, :-1]

        def _wkv(w, u, k, v):

            def step(carry, kv_t):
                aa, bb, pp = carry
                kt, vt = kv_t
                ww = u + kt
                p = jnp.maximum(pp, ww)
                e1 = jnp.exp(pp - p)
                e2 = jnp.exp(ww - p)
                y = (e1 * aa + e2 * vt) / (e1 * bb + e2)
                ww2 = pp + w
                p2 = jnp.maximum(ww2, kt)
                e1 = jnp.exp(ww2 - p2)
                e2 = jnp.exp(kt - p2)
                return ((e1 * aa + e2 * vt, e1 * bb + e2, p2), y)
            Bz, Tz, Cz = k.shape
            init = (jnp.zeros((Bz, Cz), k.dtype), jnp.zeros((Bz, Cz), k.dtype), jnp.full((Bz, Cz), -1e+38, k.dtype))
            kT = jnp.swapaxes(k, 0, 1)
            vT = jnp.swapaxes(v, 0, 1)
            _, y = jax.lax.scan(step, init, (kT, vT))
            return jnp.swapaxes(y, 0, 1)
        x = _ln(x, ln0_w, ln0_b)
        h = _ln(x, ln1_w, ln1_b)
        xx = _time_shift(h)
        xk = h * tmk + xx * (1 - tmk)
        xv = h * tmv + xx * (1 - tmv)
        xr = h * tmr + xx * (1 - tmr)
        k = jnp.einsum('btc,oc->bto', xk, Wk)
        v = jnp.einsum('btc,oc->bto', xv, Wv)
        sr = jax.nn.sigmoid(jnp.einsum('btc,oc->bto', xr, Wr))
        w = -jnp.exp(time_decay)
        att = _wkv(w, time_first, k, v)
        rwkv = jnp.einsum('btc,oc->bto', sr * att, Wo)
        x = x + rwkv
        h2 = _ln(x, ln2_w, ln2_b)
        xx2 = _time_shift(h2)
        xk2 = h2 * cmk + xx2 * (1 - cmk)
        xr2 = h2 * cmr + xx2 * (1 - cmr)
        kf = jnp.einsum('btc,hc->bth', xk2, Wfk)
        kf = jnp.square(jax.nn.relu(kf))
        kv = jnp.einsum('bth,ch->btc', kf, Wfv)
        rkv = jax.nn.sigmoid(jnp.einsum('btc,oc->bto', xr2, Wfr)) * kv
        return x + rkv

    def _L0_ffn_ref(x, We, be, Wg, bg):
        import jax, jax.numpy as jnp
        import numpy as np
        B, S, D = (4, 256, 128)
        O = 128
        E = 8
        K = 2
        b, s, d = x.shape
        x_flat = x.reshape(-1, d)
        gates = jax.nn.softmax(x_flat @ Wg + bg, axis=-1)
        topk_gates, topk_idx = jax.lax.top_k(gates, K)
        topk_gates = topk_gates / jnp.sum(topk_gates, axis=1, keepdims=True)
        expert_out = jnp.einsum('nd,edo->neo', x_flat, We) + be
        selected = jnp.take_along_axis(expert_out, topk_idx[:, :, None], axis=1)
        out = jnp.sum(selected * topk_gates[:, :, None], axis=1)
        return out.reshape(b, s, -1)
    x = L0_attn_x
    x = x + 0.5 * _L0_ffn_ref(_layernorm(x, axis=-1), L0_ffn_We, L0_ffn_be, L0_ffn_Wg, L0_ffn_bg)
    x = x + _L0_attn_ref(_layernorm(x, axis=-1), L0_attn_ln0_w, L0_attn_ln0_b, L0_attn_ln1_w, L0_attn_ln1_b, L0_attn_ln2_w, L0_attn_ln2_b, L0_attn_time_decay, L0_attn_time_first, L0_attn_tmk, L0_attn_tmv, L0_attn_tmr, L0_attn_Wk, L0_attn_Wv, L0_attn_Wr, L0_attn_Wo, L0_attn_cmk, L0_attn_cmr, L0_attn_Wfk, L0_attn_Wfr, L0_attn_Wfv)
    x = x + 0.5 * _L0_ffn_ref(_layernorm(x, axis=-1), L0_ffn_We, L0_ffn_be, L0_ffn_Wg, L0_ffn_bg)
    return x

_drawn_inputs = setup_inputs


def setup_inputs(seed=0):
    import zlib

    import numpy as np

    out = dict(_drawn_inputs(seed))
    spreads = {'L0_attn_ln0_w': (1.0, 0.2),
     'L0_attn_ln0_b': (0.0, 0.1),
     'L0_attn_ln1_w': (1.0, 0.6),
     'L0_attn_ln1_b': (0.0, 0.8),
     'L0_attn_ln2_w': (1.0, 0.6),
     'L0_attn_ln2_b': (0.0, 0.8)}
    factors = {'L0_attn_time_decay': 7.273,
     'L0_attn_time_first': 8.0,
     'L0_attn_tmk': 8.0,
     'L0_attn_tmv': 8.0,
     'L0_attn_tmr': 8.0,
     'L0_attn_Wk': 8.0,
     'L0_attn_Wv': 5.788,
     'L0_attn_Wr': 8.0,
     'L0_attn_Wo': 5.855,
     'L0_attn_cmk': 8.0,
     'L0_attn_cmr': 8.0,
     'L0_attn_Wfk': 8.0,
     'L0_attn_Wfr': 8.0,
     'L0_attn_Wfv': 7.687}
    for name, (base, spread) in spreads.items():
        noise = np.random.default_rng([zlib.crc32(name.encode()), seed]).standard_normal(out[name].shape)
        drawn = base * np.exp(spread * noise) if base else spread * noise
        out[name] = jnp.asarray(drawn.astype(out[name].dtype))
    for name, factor in factors.items():
        out[name] = (out[name] * factor).astype(out[name].dtype)
    return out
```

```python
from contextlib import ExitStack

import concourse.bass as bass
from concourse import mybir

ALU = mybir.AluOpType
ACT = mybir.ActivationFunctionType
AX_X = mybir.AxisListType.X
F32 = mybir.dt.float32

C = 128
BATCHES = 4
TOK = 512
TILES = TOK // C
E = 8
HALF = E // 2
HC = 4
EPS = 1e-5
LOWEST = -1e38
NEVER = -3.4e38

V_DECAY, V_FIRST, V_TMK, V_TMV, V_TMR, V_LN1W, V_LN1B, V_LN2W, V_LN2B, V_CMK, V_CMR = range(11)
NV = 11


def macaron_kernel(nc, x, vectors, ln0_w, ln0_b, w_att, w_ffn_k, w_ffn_v, w_exp, b_exp, w_gate, b_gate, ident_in, out):
    with ExitStack() as ctx:
        def sb(name, *shape):
            return ctx.enter_context(nc.sbuf_tensor(name, list(shape), F32))

        def sem(name):
            return ctx.enter_context(nc.semaphore(name))

        X = sb("X", C, BATCHES * TOK)
        X1 = sb("X1", C, BATCHES * TOK)
        X0 = sb("X0", C, BATCHES * TOK)
        X2 = sb("X2", C, BATCHES * TOK)
        Y = sb("Y", C, BATCHES * TOK)
        ident = sb("ident", C, C)
        vec = sb("vec", C, NV)
        w0b = sb("w0b", C, C)
        b0b = sb("b0b", C, C)
        watt = sb("watt", C, 5 * C)
        wfk = sb("wfk", C, HC * C)
        wfv = sb("wfv", C, HC * C)
        wexp = sb("wexp", C, E * C)
        bexp = sb("bexp", TILES * E, TILES * C)
        wgate = sb("wgate", C, E)
        bgate = sb("bgate", C, TILES * E)
        mhalf = sb("mhalf", C, TILES)
        decay = sb("decay", C, 1)
        decay_w = sb("decay_w", C, TOK)
        stats = sb("stats", C, TILES * 6)
        mv = sb("mv", C, TILES * 2)
        rstd = sb("rstd", C, TILES)
        vtmp = sb("vtmp", C, TILES)
        xn = sb("xn", C, TOK)
        xnT = sb("xnT", C, TOK)
        logit = sb("logit", C, TILES * E)
        top = sb("top", C, TILES * E)
        top2 = sb("top2", C, TILES * E)
        rest = sb("rest", C, TILES * E)
        shifted = sb("shifted", C, TILES * E)
        expo = sb("expo", C, TILES * E)
        chosen = sb("chosen", C, TILES * E)
        gsum = sb("gsum", C, TILES)
        ginv = sb("ginv", C, TILES)
        gate = sb("gate", C, TILES * E)
        gateT = sb("gateT", TILES * E, C)
        base = sb("base", C, TOK)
        acc = sb("acc", C, 2 * C)
        prod = sb("prod", C, 2 * HALF * C)
        pair = sb("pair", C, 2 * C)
        psum1 = sb("psum1", C, C)
        n2 = sb("n2", C, TOK)
        t0 = sb("t0", C, TOK)
        stats2 = sb("stats2", C, TILES * 6)
        mv2 = sb("mv2", C, TILES * 2)
        stats3 = sb("stats3", C, TILES * 6)
        mv3 = sb("mv3", C, TILES * 2)
        rstd2 = sb("rstd2", C, TILES)
        vtmp2 = sb("vtmp2", C, TILES)
        rstd3 = sb("rstd3", C, TILES)
        vtmp3 = sb("vtmp3", C, TILES)
        n1 = sb("n1", C, TOK)
        h1 = sb("h1", C, TOK + 1)
        dh = sb("dh", C, TOK)
        xk = sb("xk", C, TOK)
        xv = sb("xv", C, TOK)
        xr = sb("xr", C, TOK)
        kS = sb("kS", C, TOK)
        vS = sb("vS", C, TOK)
        th = sb("th", C, TOK)
        PP = sb("PP", C, TOK + 1)
        q = sb("q", C, TOK)
        qq = sb("qq", C, 2 * TOK)
        de = sb("de", C, 2 * TOK)
        z = sb("z", C, TOK)
        zz = sb("zz", C, 2 * TOK)
        e12 = sb("e12", C, 3 * TOK)
        ev = sb("ev", C, TOK)
        AB = sb("AB", C, 2 * (TOK + 1))
        nd0 = sb("nd0", C, 2 * TOK)
        nd = sb("nd", C, 2 * TOK)
        rden = sb("rden", C, TOK)
        att = sb("att", C, TOK)
        sa = sb("sa", C, TOK)
        XR = sb("XR", C, TOK)
        xs = sb("xs", C, TOK)
        n3 = sb("n3", C, TOK)
        h2 = sb("h2", C, TOK + 1)
        dh2 = sb("dh2", C, TOK)
        xk2 = sb("xk2", C, TOK)
        xr2 = sb("xr2", C, TOK)
        rl = sb("rl", C, 2 * TOK)
        kf = sb("kf", C, HC * TOK)
        th2 = sb("th2", C, TOK)
        rkv = sb("rkv", C, TOK)

        bank = [ctx.enter_context(nc.psum_tensor(f"bank{i}", [C, TOK], F32)) for i in range(8)]
        ps_exp = [bank[0], bank[2]], [bank[1], bank[3]]
        ps_xT, ps_gate, ps_base = bank[4], bank[5], bank[6]
        ps_k, ps_v, ps_r, ps_o = bank[0], bank[1], bank[2], bank[3]
        ps_hT, ps_h2T = bank[4], bank[7]
        ps_kf = [bank[5], bank[6]]
        ps_r2, ps_kv = bank[7], bank[3]

        s_x0 = sem("x_first_loaded")
        s_xr = sem("x_rest_loaded")
        s_id = sem("ident_loaded")
        s_wg = sem("gate_weights_loaded")
        s_we = sem("expert_weights_loaded")
        s_be = sem("expert_biases_loaded")
        s_vec = sem("vectors_loaded")
        s_wa = sem("attention_weights_loaded")
        s_z = sem("bias_block_zeroed")
        s_const = sem("pool_constants_set")
        s_pres = sem("dve_constants_set")
        s_dec = sem("decay_exponential")
        s_out = sem("output_stored")

        s_passed_dve = sem("dve_wait_passed")
        s_passed_pool = sem("pool_wait_passed")

        MOE = ("stats", "meanvar", "var_eps", "rstd", "norm", "xT", "xT_copied", "logits", "gate_step",
               "shifted", "exp", "gateT", "gateT_copied", "bias", "base", "exp_lo", "exp_hi", "combine",
               "scaled", "pair", "psum1", "out")
        ATT = ("stats", "meanvar", "var_eps", "rstd", "n2", "x0_step", "stats2", "meanvar2", "var2_eps", "rstd2",
               "n1", "hT", "h1", "diff", "mixed", "k", "v", "r", "k_copied", "v_copied", "th",
               "qq", "de", "zz", "e12", "e2v", "wkv", "sa", "o", "XR", "stats3", "meanvar3", "var3_eps", "rstd3",
               "n3", "h2T", "h2", "diff2", "mixed2", "kf", "relu", "kf2", "r2", "th2", "kv", "xs", "rkv", "out")
        moe = [{n: sem(f"moe{f}_{n}") for n in MOE} for f in range(2)]
        a = {n: sem(f"att_{n}") for n in ATT}

        SRC, DST = (X, X2), (X1, Y)
        G = 9
        W = 10

        def seq(t, b, lo=0, n=TOK):
            return t[:, bass.ds(b * TOK + lo, n)]

        def grp(ap, n):
            return ap.rearrange("p (t n) -> p t n", n=n)

        def wait_if(eng, s, v):
            if not isinstance(v, int) or v > 0:
                eng.wait_ge(s, v)

        block = ctx.enter_context(nc.Block())

        @block.sync
        def _(sp):
            xin = x.rearrange("(b t p) c -> p b t c", t=TILES, p=C)
            dst = X[:, :].rearrange("p (b t c) -> p b t c", b=BATCHES, t=TILES)
            sp.dma_start(dst[:, 0], xin[:, 0]).then_inc(s_x0, 16)
            sp.dma_start(wgate[:, :], w_gate).then_inc(s_wg, 16)
            sp.dma_start(bgate[:, :], b_gate).then_inc(s_wg, 16)
            for b in range(1, BATCHES):
                sp.dma_start(dst[:, b], xin[:, b]).then_inc(s_xr, 16)
            sp.dma_start(vec[:, :], vectors).then_inc(s_vec, 16)
            sp.dma_start(w0b[:, :], ln0_w.partition_broadcast(C)).then_inc(s_vec, 16)
            sp.dma_start(b0b[:, :], ln0_b.partition_broadcast(C)).then_inc(s_vec, 16)
            yout = out.rearrange("(b t p) c -> p b t c", t=TILES, p=C)
            ysb = Y[:, :].rearrange("p (b t c) -> p b t c", b=BATCHES, t=TILES)
            for b in range(BATCHES):
                sp.wait_ge(moe[1]["out"], TILES * (b + 1))
                sp.dma_start(yout[:, b], ysb[:, b]).then_inc(s_out, 16)
            sp.wait_ge(s_out, 16 * BATCHES)

        @block.tensor
        def _(pe):
            def moe_transposes(f, b):
                m = moe[f]
                wait_if(pe, m["xT_copied"], TILES * b)
                for t in range(TILES):
                    pe.wait_ge(m["norm"], TILES * b + t + 1)
                    mm = pe.transpose(ps_xT[:, t * C:(t + 1) * C], xn[:, t * C:(t + 1) * C], ident[:, :])
                mm.then_inc(m["xT"], 1)

            def moe_logits(f, b):
                m = moe[f]
                wait_if(pe, m["gateT_copied"], b)
                for t in range(TILES):
                    pe.wait_ge(m["xT_copied"], TILES * b + t + 1)
                    mm = pe.matmul(ps_gate[:, t * E:(t + 1) * E], xnT[:, t * C:(t + 1) * C], wgate[:, :],
                                   start=True, stop=True)
                mm.then_inc(m["logits"], 1)

            def moe_bias(f, b):
                m = moe[f]
                pe.wait_ge(m["gate_step"], G * b + G)
                pe.transpose(ps_gate[0:TILES * E, C:2 * C], gate[:, :], ident[:, :]).then_inc(m["gateT"], 1)
                pe.wait_ge(m["gateT_copied"], b + 1)
                wait_if(pe, m["base"], b)
                pe.matmul(ps_base[:, :], gateT[:, :], bexp[:, :], start=True, stop=True).then_inc(m["bias"], 1)

            def moe_experts(f, b, t):
                m = moe[f]
                n = TILES * b + t
                for half, (done, freed, per) in enumerate(((m["exp_lo"], m["combine"], HALF), (m["exp_hi"], m["scaled"], 1))):
                    if not isinstance(b, int) or n >= 2:
                        pe.wait_ge(freed, (n - 1) * per)
                    pe.matmul(ps_exp[half][t % 2][:, :], xnT[:, t * C:(t + 1) * C],
                              wexp[:, half * HALF * C:(half + 1) * HALF * C], start=True, stop=True).then_inc(done, 1)

            def moe_body(f, b, last):
                moe_experts(f, b, 0)
                moe_experts(f, b, 1)
                moe_bias(f, b)
                moe_experts(f, b, 2)
                if not last:
                    moe_transposes(f, b + 1)
                moe_experts(f, b, 3)
                if not last:
                    moe_logits(f, b + 1)

            def moe_phase(f):
                moe_transposes(f, 0)
                moe_logits(f, 0)
                moe_body(f, 0, False)
                with pe.Fori(1, BATCHES - 1) as b:
                    moe_body(f, b, False)
                moe_body(f, BATCHES - 1, True)

            def att_transpose(b):
                wait_if(pe, a["h1"], b)
                for t in range(TILES):
                    pe.wait_ge(a["n1"], TILES * b + t + 1)
                    mm = pe.transpose(ps_hT[:, t * C:(t + 1) * C], n1[:, t * C:(t + 1) * C], ident[:, :])
                mm.then_inc(a["hT"], 1)

            def att_kvr(b):
                for i, (ps, src, done, freed) in enumerate(((ps_k, xk, a["k"], a["k_copied"]), (ps_v, xv, a["v"], a["v_copied"]),
                                                            (ps_r, xr, a["r"], a["th"]))):
                    wait_if(pe, freed, b)
                    pe.wait_ge(a["mixed"], 3 * b + i + 1)
                    pe.matmul(ps[:, :], watt[:, i * C:(i + 1) * C], src[:, :], start=True, stop=True).then_inc(done, 1)

            def att_o(b):
                wait_if(pe, a["rkv"], b)
                pe.wait_ge(a["sa"], b + 1)
                for t in range(TILES):
                    mm = pe.matmul(ps_o[:, t * C:(t + 1) * C], sa[:, t * C:(t + 1) * C], watt[:, 3 * C:4 * C],
                                   start=True, stop=True)
                mm.then_inc(a["o"], 1)

            def att_transpose2(b):
                wait_if(pe, a["th2"], b)
                for t in range(TILES):
                    pe.wait_ge(a["n3"], TILES * b + t + 1)
                    mm = pe.transpose(ps_h2T[:, t * C:(t + 1) * C], n3[:, t * C:(t + 1) * C], ident[:, :])
                mm.then_inc(a["h2T"], 1)

            def att_kf(b):
                for j in range(HC):
                    if j >= 2:
                        pe.wait_ge(a["relu"], HC * b + j - 1)
                    else:
                        wait_if(pe, a["relu"], HC * b)
                    if j == 0:
                        pe.wait_ge(a["mixed2"], 2 * b + 1)
                    pe.matmul(ps_kf[j % 2][:, :], wfk[:, j * C:(j + 1) * C], xk2[:, :],
                              start=True, stop=True).then_inc(a["kf"], 1)

            def att_r2(b):
                pe.wait_ge(a["mixed2"], 2 * b + 2)
                pe.wait_ge(a["h2"], b + 1)
                for t in range(TILES):
                    mm = pe.matmul(ps_r2[:, t * C:(t + 1) * C], xr2[:, t * C:(t + 1) * C], watt[:, 4 * C:5 * C],
                                   start=True, stop=True)
                mm.then_inc(a["r2"], 1)

            def att_kv(b):
                pe.wait_ge(a["XR"], b + 1)
                pe.wait_ge(a["kf2"], HC * b + HC)
                for t in range(TILES):
                    for j in range(HC):
                        mm = pe.matmul(ps_kv[:, t * C:(t + 1) * C], kf[:, j * TOK + t * C:j * TOK + (t + 1) * C],
                                       wfv[:, j * C:(j + 1) * C], start=(j == 0), stop=(j == HC - 1))
                mm.then_inc(a["kv"], 1)

            pe.wait_ge(s_id, 16)
            pe.wait_ge(s_wg, 32)
            pe.wait_ge(s_we, 16)
            pe.wait_ge(s_be, 16 * TILES)
            moe_phase(0)

            pe.wait_ge(s_wa, 48)
            pe.wait_ge(moe[0]["combine"], HALF * TILES * BATCHES)
            pe.wait_ge(moe[0]["scaled"], TILES * BATCHES)
            att_transpose(0)
            att_kvr(0)
            pe.wait_ge(moe[0]["base"], BATCHES)
            def att_body(b):
                att_o(b - 1)
                att_transpose(b)
                att_kvr(b)
                att_transpose2(b - 1)
                att_kf(b - 1)
                att_r2(b - 1)
                att_kv(b - 1)

            att_body(1)
            with pe.Fori(2, BATCHES) as b:
                att_body(b)
            att_o(BATCHES - 1)
            att_transpose2(BATCHES - 1)
            att_kf(BATCHES - 1)
            att_r2(BATCHES - 1)
            att_kv(BATCHES - 1)

            pe.wait_ge(a["relu"], HC * BATCHES)
            pe.wait_ge(a["rkv"], BATCHES)
            moe_phase(1)

        @block.vector
        def _(dve):
            def settled():
                dve.sem_inc(s_passed_dve, 1)

            def layer_stats(src, st, out2, s_stats, s_mv, b):
                settled()
                for t in range(TILES):
                    i = dve.bn_stats(st[:, t * 6:(t + 1) * 6], src(t))
                i.then_inc(s_stats, 1)
                dve.wait_ge(s_stats, b + 1)
                settled()
                for t in range(TILES):
                    i = dve.bn_aggr(out2[:, t * 2:(t + 1) * 2], st[:, t * 6:(t + 1) * 6])
                i.then_inc(s_mv, 1)

            def normalise(dst, src, out2, rs, s_rs, s_out, s_free, b):
                dve.wait_ge(s_rs, b + 1)
                for t in range(TILES):
                    wait_if(dve, s_free, b)
                    dve.tensor_scalar(dst[:, t * C:(t + 1) * C], src(t), out2[:, 2 * t:2 * t + 1], rs[:, t:t + 1],
                                      ALU.subtract, ALU.mult).then_inc(s_out, 1)

            def moe_norm(f, b):
                m = moe[f]

                def src(t):
                    return seq(SRC[f], b, t * C, C)
                if f == 0:
                    if isinstance(b, int) and b == 0:
                        dve.wait_ge(s_x0, 16)
                    else:
                        dve.wait_ge(s_xr, 16 * (BATCHES - 1))
                else:
                    dve.wait_ge(a["out"], b + 1)
                layer_stats(src, stats, mv, m["stats"], m["meanvar"], b)
                dve.wait_ge(m["rstd"], b + 1)
                for t in range(TILES):
                    wait_if(dve, m["xT"], b)
                    dve.tensor_scalar(xn[:, t * C:(t + 1) * C], src(t), mv[:, 2 * t:2 * t + 1], rstd[:, t:t + 1],
                                      ALU.subtract, ALU.mult).then_inc(m["norm"], 1)

            def moe_gates(f, b):
                m = moe[f]

                def step(k):
                    dve.wait_ge(m["gate_step"], G * b + k)
                dve.wait_ge(m["logits"], b + 1)
                if f == 0:
                    dve.wait_ge(s_wg, 32)
                dve.tensor_tensor(logit[:, :], ps_gate[:, 0:TILES * E], bgate[:, :], ALU.add).then_inc(m["gate_step"], 1)
                step(1)
                settled()
                for t in range(TILES):
                    i = dve.max(top[:, t * E:(t + 1) * E], logit[:, t * E:(t + 1) * E])
                i.then_inc(m["gate_step"], 1)
                step(2)
                dve.tensor_copy(grp(top2[:, :], E)[:, :, 0:2], grp(top[:, :], E)[:, :, 0:2]).then_inc(m["gate_step"], 1)
                dve.tensor_tensor(grp(shifted[:, :], E), grp(logit[:, :], E),
                                  grp(top[:, :], E)[:, :, 0:1].to_broadcast([C, TILES, E]),
                                  ALU.subtract).then_inc(m["shifted"], 1)
                step(3)
                settled()
                for t in range(TILES):
                    s = slice(t * E, (t + 1) * E)
                    i = dve.match_replace(rest[:, s], top2[:, s], logit[:, s], NEVER)
                i.then_inc(m["gate_step"], 1)
                step(4)
                dve.tensor_tensor(chosen[:, :], logit[:, :], rest[:, :], ALU.not_equal).then_inc(m["gate_step"], 1)
                step(5)
                dve.wait_ge(m["exp"], b + 1)
                dve.tensor_tensor(chosen[:, :], expo[:, :], chosen[:, :], ALU.mult).then_inc(m["gate_step"], 1)
                step(6)
                dve.tensor_reduce(gsum[:, :], grp(chosen[:, :], E), AX_X, ALU.add).then_inc(m["gate_step"], 1)
                step(7)
                dve.reciprocal(ginv[:, :], gsum[:, :]).then_inc(m["gate_step"], 1)
                step(8)
                wait_if(dve, m["scaled"], TILES * b)
                dve.scalar_tensor_tensor(grp(gate[:, :], E), grp(chosen[:, :], E), 0.5,
                                         ginv[:, :].unsqueeze(2).to_broadcast([C, TILES, E]),
                                         ALU.mult, ALU.mult).then_inc(m["gate_step"], 1)

            def moe_base(f, b):
                m = moe[f]
                dve.wait_ge(m["bias"], b + 1)
                dve.tensor_tensor(base[:, :], ps_base[:, :], seq(SRC[f], b), ALU.add).then_inc(m["base"], 1)
                dve.wait_ge(m["base"], b + 1)

            def moe_combine(f, b, t):
                m = moe[f]
                n = TILES * b + t
                half = acc[:, (t % 2) * C:(t % 2 + 1) * C]
                dve.wait_ge(m["exp_lo"], n + 1)
                if not isinstance(b, int) or n >= 2:
                    dve.wait_ge(m["out"], n - 1)
                for e in range(HALF):
                    if e:
                        dve.wait_ge(m["combine"], HALF * n + e)
                    dve.scalar_tensor_tensor(half, ps_exp[0][t % 2][:, e * C:(e + 1) * C],
                                             gate[:, t * E + e:t * E + e + 1],
                                             base[:, t * C:(t + 1) * C] if e == 0 else half,
                                             ALU.mult, ALU.add).then_inc(m["combine"], 1)

            def moe_body(f, b, last):
                moe_base(f, b)
                moe_combine(f, b, 0)
                if not last:
                    moe_norm(f, b + 1)
                moe_combine(f, b, 1)
                moe_combine(f, b, 2)
                moe_combine(f, b, 3)
                if not last:
                    moe_gates(f, b + 1)

            def moe_phase(f):
                moe_norm(f, 0)
                moe_gates(f, 0)
                moe_body(f, 0, False)
                with dve.Fori(1, BATCHES - 1) as b:
                    moe_body(f, b, False)
                moe_body(f, BATCHES - 1, True)

            def att_x0(b):
                def src(t):
                    return seq(X1, b, t * C, C)

                dve.wait_ge(moe[0]["out"], TILES * (b + 1))
                layer_stats(src, stats, mv, a["stats"], a["meanvar"], b)
                dve.wait_ge(a["rstd"], b + 1)
                for t in range(TILES):
                    i = dve.tensor_scalar(n2[:, t * C:(t + 1) * C], src(t), mv[:, 2 * t:2 * t + 1], rstd[:, t:t + 1],
                                          ALU.subtract, ALU.mult)
                i.then_inc(a["n2"], 1)
                dve.wait_ge(a["n2"], b + 1)
                dve.tensor_tensor(grp(t0[:, :], C), grp(n2[:, :], C),
                                  w0b[:, :].unsqueeze(1).to_broadcast([C, TILES, C]), ALU.mult).then_inc(a["x0_step"], 1)
                dve.wait_ge(a["x0_step"], 2 * b + 1)
                dve.tensor_tensor(grp(seq(X0, b), C), grp(t0[:, :], C),
                                  b0b[:, :].unsqueeze(1).to_broadcast([C, TILES, C]), ALU.add).then_inc(a["x0_step"], 1)
                dve.wait_ge(a["x0_step"], 2 * b + 2)

                def src0(t):
                    return seq(X0, b, t * C, C)
                layer_stats(src0, stats2, mv2, a["stats2"], a["meanvar2"], b)
                normalise(n1, src0, mv2, rstd2, a["rstd2"], a["n1"], a["hT"], b)

            def att_mix(b):
                dve.wait_ge(a["h1"], b + 1)
                dve.tensor_tensor(dh[:, :], h1[:, 1:TOK + 1], h1[:, 0:TOK], ALU.subtract).then_inc(a["diff"], 1)
                dve.wait_ge(a["diff"], b + 1)
                for dst, col, used in ((xk, V_TMK, a["k"]), (xv, V_TMV, a["v"]), (xr, V_TMR, a["r"])):
                    wait_if(dve, used, b)
                    dve.scalar_tensor_tensor(dst[:, :], dh[:, :], vec[:, col:col + 1], h1[:, 0:TOK],
                                             ALU.mult, ALU.add).then_inc(a["mixed"], 1)

            def att_wkv(b):
                def step(k):
                    dve.wait_ge(a["wkv"], W * b + k)

                def done(i):
                    i.then_inc(a["wkv"], 1)
                lo, hi = slice(0, TOK), slice(TOK, 2 * TOK)
                dve.wait_ge(a["k_copied"], b + 1)
                done(dve.tensor_tensor_scan(PP[:, 1:TOK + 1], decay_w[:, :], kS[:, :], LOWEST, ALU.add, ALU.max))
                step(1)
                done(dve.scalar_tensor_tensor(q[:, :], PP[:, 0:TOK], decay[:, 0:1], kS[:, :], ALU.add, ALU.subtract))
                done(dve.scalar_tensor_tensor(z[:, :], kS[:, :], vec[:, V_FIRST:V_FIRST + 1], PP[:, 0:TOK],
                                              ALU.add, ALU.subtract))
                step(2)
                wait_if(dve, a["de"], b)
                dve.tensor_scalar(qq[:, lo], q[:, :], 0.0, None, ALU.min).then_inc(a["qq"], 1)
                dve.tensor_scalar(qq[:, hi], q[:, :], -1.0, 0.0, ALU.mult, ALU.min).then_inc(a["qq"], 1)
                step(3)
                dve.tensor_scalar(zz[:, lo], z[:, :], -1.0, 0.0, ALU.mult, ALU.min).then_inc(a["zz"], 1)
                dve.tensor_scalar(zz[:, hi], z[:, :], 0.0, None, ALU.min).then_inc(a["zz"], 1)
                dve.wait_ge(a["de"], b + 1)
                dve.wait_ge(a["v_copied"], b + 1)
                done(dve.tensor_tensor(ev[:, :], de[:, hi], vS[:, :], ALU.mult))
                done(dve.tensor_tensor_scan(AB[:, TOK + 2:2 * TOK + 2], de[:, lo], de[:, hi], 0.0, ALU.mult, ALU.add))
                step(4)
                done(dve.tensor_tensor_scan(AB[:, 1:TOK + 1], de[:, lo], ev[:, :], 0.0, ALU.mult, ALU.add))
                step(6)
                dve.wait_ge(a["e12"], b + 1)
                ab = AB[:, :].rearrange("p (s n) -> p s n", s=2)[:, :, 0:TOK]
                done(dve.tensor_tensor(grp(nd0[:, :], TOK), ab, e12[:, lo].unsqueeze(1).to_broadcast([C, 2, TOK]),
                                       ALU.mult))
                step(7)
                dve.wait_ge(a["e2v"], b + 1)
                done(dve.tensor_tensor(nd[:, :], nd0[:, :], e12[:, TOK:3 * TOK], ALU.add))
                step(8)
                done(dve.reciprocal(rden[:, :], nd[:, hi]))
                step(9)
                done(dve.tensor_tensor(att[:, :], nd[:, lo], rden[:, :], ALU.mult))
                step(10)
                dve.wait_ge(a["th"], b + 1)
                wait_if(dve, a["o"], b)
                dve.scalar_tensor_tensor(sa[:, :], th[:, :], 1.0, att[:, :], ALU.add, ALU.mult).then_inc(a["sa"], 1)

            def att_resid(b):
                dve.wait_ge(a["o"], b + 1)
                wait_if(dve, a["xs"], b)
                dve.scalar_tensor_tensor(XR[:, :], ps_o[:, :], 0.5, seq(X0, b), ALU.mult, ALU.add).then_inc(a["XR"], 1)
                dve.wait_ge(a["XR"], b + 1)

                def src(t):
                    return XR[:, t * C:(t + 1) * C]
                layer_stats(src, stats3, mv3, a["stats3"], a["meanvar3"], b)
                normalise(n3, src, mv3, rstd3, a["rstd3"], a["n3"], a["h2T"], b)

            def att_mix2(b):
                dve.wait_ge(a["h2"], b + 1)
                dve.tensor_tensor(dh2[:, :], h2[:, 1:TOK + 1], h2[:, 0:TOK], ALU.subtract).then_inc(a["diff2"], 1)
                dve.wait_ge(a["diff2"], b + 1)
                wait_if(dve, a["kf"], HC * b)
                dve.scalar_tensor_tensor(xk2[:, :], dh2[:, :], vec[:, V_CMK:V_CMK + 1], h2[:, 0:TOK],
                                         ALU.mult, ALU.add).then_inc(a["mixed2"], 1)
                wait_if(dve, a["r2"], b)
                dve.scalar_tensor_tensor(xr2[:, :], dh2[:, :], vec[:, V_CMR:V_CMR + 1], h2[:, 0:TOK],
                                         ALU.mult, ALU.add).then_inc(a["mixed2"], 1)

            def att_out(b):
                dve.wait_ge(a["kv"], b + 1)
                dve.wait_ge(a["th2"], b + 1)
                dve.scalar_tensor_tensor(rkv[:, :], th2[:, :], 1.0, ps_kv[:, :], ALU.add, ALU.mult).then_inc(a["rkv"], 1)
                dve.wait_ge(a["rkv"], b + 1)
                dve.wait_ge(a["xs"], b + 1)
                dve.scalar_tensor_tensor(seq(X2, b), rkv[:, :], 0.5, xs[:, :], ALU.mult, ALU.add).then_inc(a["out"], 1)

            for t, v in ((top2[:, :], NEVER), (h1[:, 0:1], 0.0), (h2[:, 0:1], 0.0), (PP[:, 0:1], LOWEST),
                         (AB[:, 0:1], 0.0), (AB[:, TOK + 1:TOK + 2], 0.0)):
                dve.memset(t, v).then_inc(s_pres, 1)
            dve.memset(decay_w[:, :], 0.0).then_inc(s_pres, 1)
            dve.wait_ge(s_pres, 7)
            moe_phase(0)

            dve.wait_ge(s_vec, 48)
            dve.wait_ge(s_dec, 1)
            dve.tensor_scalar(decay[:, :], decay[:, :], -1.0, None, ALU.mult).then_inc(s_dec, 1)
            dve.wait_ge(s_dec, 2)
            dve.tensor_scalar(decay_w[:, :], decay_w[:, :], decay[:, 0:1], None, ALU.add).then_inc(s_dec, 1)
            dve.wait_ge(s_dec, 3)
            att_x0(0)
            att_mix(0)
            att_wkv(0)
            def att_body(b):
                att_x0(b)
                att_resid(b - 1)
                att_mix(b)
                att_mix2(b - 1)
                att_wkv(b)
                att_out(b - 1)

            att_body(1)
            with dve.Fori(2, BATCHES) as b:
                att_body(b)
            att_resid(BATCHES - 1)
            att_mix2(BATCHES - 1)
            att_out(BATCHES - 1)

            moe_phase(1)

        @block.scalar
        def _(act):
            def moe_copy_xT(f, b, t):
                m = moe[f]
                act.wait_ge(m["xT"], b + 1)
                wait_if(act, m["exp_hi"], (TILES * (b - 1) + t + 1) if not isinstance(b, int) or b else 0)
                act.copy(xnT[:, t * C:(t + 1) * C], ps_xT[:, t * C:(t + 1) * C]).then_inc(m["xT_copied"], 1)

            def moe_exp(f, b):
                m = moe[f]
                act.wait_ge(m["shifted"], b + 1)
                act.activation(expo[:, :], shifted[:, :], ACT.Exp).then_inc(m["exp"], 1)
                act.wait_ge(m["gateT"], b + 1)
                wait_if(act, m["bias"], b)
                act.copy(gateT[:, :], ps_gate[0:TILES * E, C:2 * C]).then_inc(m["gateT_copied"], 1)

            def moe_scale(f, b, t):
                m = moe[f]
                n = TILES * b + t
                if t == 0:
                    act.wait_ge(m["gate_step"], G * b + G)
                act.wait_ge(m["exp_hi"], n + 1)
                if not isinstance(b, int) or n >= 2:
                    act.wait_ge(m["pair"], n - 1)
                for e in range(HALF):
                    o = ((t % 2) * HALF + e) * C
                    i = act.activation(prod[:, o:o + C], ps_exp[1][t % 2][:, e * C:(e + 1) * C], ACT.Copy,
                                       scale=gate[:, t * E + HALF + e:t * E + HALF + e + 1])
                i.then_inc(m["scaled"], 1)

            def moe_body(f, b):
                for t in range(TILES - 1):
                    moe_scale(f, b, t)
                for t in range(TILES - 1):
                    moe_copy_xT(f, b + 1, t)
                moe_scale(f, b, TILES - 1)
                moe_copy_xT(f, b + 1, TILES - 1)
                moe_exp(f, b + 1)

            def moe_phase(f):
                for t in range(TILES):
                    moe_copy_xT(f, 0, t)
                moe_exp(f, 0)
                moe_body(f, 0)
                with act.Fori(1, BATCHES - 1) as b:
                    moe_body(f, b)
                for t in range(TILES):
                    moe_scale(f, BATCHES - 1, t)

            def att_h1(b):
                act.wait_ge(a["hT"], b + 1)
                wait_if(act, a["mixed"], 3 * b)
                act.activation(h1[:, 1:TOK + 1], ps_hT[:, :], ACT.Identity, bias=vec[:, V_LN1B:V_LN1B + 1],
                               scale=vec[:, V_LN1W:V_LN1W + 1]).then_inc(a["h1"], 1)

            def att_kvr(b):
                act.wait_ge(a["k"], b + 1)
                wait_if(act, a["sa"], b)
                act.copy(kS[:, :], ps_k[:, :]).then_inc(a["k_copied"], 1)
                act.wait_ge(a["v"], b + 1)
                act.copy(vS[:, :], ps_v[:, :]).then_inc(a["v_copied"], 1)
                act.wait_ge(a["r"], b + 1)
                act.activation(th[:, :], ps_r[:, :], ACT.Tanh, scale=0.5).then_inc(a["th"], 1)

            def att_exps(b):
                act.wait_ge(a["qq"], 2 * b + 2)
                act.activation(de[:, :], qq[:, :], ACT.Exp).then_inc(a["de"], 1)
                act.wait_ge(a["zz"], 2 * b + 2)
                act.activation(e12[:, :].rearrange("p (s n) -> p s n", s=3)[:, 0:3:2, :], grp(zz[:, :], TOK),
                               ACT.Exp).then_inc(a["e12"], 1)

            def att_h2(b):
                act.wait_ge(a["h2T"], b + 1)
                wait_if(act, a["mixed2"], 2 * b)
                act.activation(h2[:, 1:TOK + 1], ps_h2T[:, :], ACT.Identity, bias=vec[:, V_LN2B:V_LN2B + 1],
                               scale=vec[:, V_LN2W:V_LN2W + 1]).then_inc(a["h2"], 1)

            def att_relu(b, j):
                act.wait_ge(a["kf"], HC * b + j + 1)
                if j >= 2:
                    act.wait_ge(a["kf2"], HC * b + j - 1)
                else:
                    wait_if(act, a["kf2"], HC * b)
                o = (j % 2) * TOK
                act.activation(rl[:, o:o + TOK], ps_kf[j % 2][:, :], ACT.Relu).then_inc(a["relu"], 1)

            def att_th2(b):
                act.wait_ge(a["r2"], b + 1)
                wait_if(act, a["rkv"], b)
                act.activation(th2[:, :], ps_r2[:, :], ACT.Tanh, scale=0.5).then_inc(a["th2"], 1)

            act.dma_start(ident[:, :], ident_in).then_inc(s_id, 16)
            act.dma_start(wexp[:, :], w_exp).then_inc(s_we, 16)
            act.wait_ge(s_z, 1)
            for t in range(TILES):
                act.dma_start(bexp[t * E:(t + 1) * E, t * C:(t + 1) * C], b_exp).then_inc(s_be, 16)
            act.dma_start(watt[:, :], w_att).then_inc(s_wa, 16)
            act.dma_start(wfk[:, :], w_ffn_k).then_inc(s_wa, 16)
            act.dma_start(wfv[:, :], w_ffn_v).then_inc(s_wa, 16)
            moe_phase(0)

            act.wait_ge(s_vec, 48)
            act.activation(decay[:, :], vec[:, V_DECAY:V_DECAY + 1], ACT.Exp).then_inc(s_dec, 1)
            act.wait_ge(s_pres, 7)
            att_h1(0)
            att_kvr(0)
            att_exps(0)
            def att_body(b):
                att_h1(b)
                att_h2(b - 1)
                att_kvr(b)
                att_relu(b - 1, 0)
                att_relu(b - 1, 1)
                att_exps(b)
                att_relu(b - 1, 2)
                att_relu(b - 1, 3)
                att_th2(b - 1)

            att_body(1)
            with act.Fori(2, BATCHES) as b:
                att_body(b)
            att_h2(BATCHES - 1)
            for j in range(HC):
                att_relu(BATCHES - 1, j)
            att_th2(BATCHES - 1)

            moe_phase(1)

        @block.gpsimd
        def _(pool):
            def inverse_root(dst, tmp, out2, scale, add, s_mv, s_tmp, s_dst, b, s_read, n_read):
                pool.wait_ge(s_mv, b + 1)
                wait_if(pool, s_read, n_read)
                pool.sem_inc(s_passed_pool, 1)
                pool.tensor_scalar(tmp[:, :], grp(out2[:, :], 2)[:, :, 1], scale, add, ALU.mult,
                                   ALU.add).then_inc(s_tmp, 1)
                pool.wait_ge(s_tmp, b + 1)
                pool.tensor_tensor(dst[:, :], tmp[:, :], mhalf[:, :], ALU.pow).then_inc(s_dst, 1)

            def moe_rstd(f, b):
                m = moe[f]
                inverse_root(rstd, vtmp, mv, 1.0, EPS, m["meanvar"], m["var_eps"], m["rstd"], b, m["norm"], TILES * b)

            def moe_sum(f, b, t):
                m = moe[f]
                n = TILES * b + t
                o = (t % 2) * HALF * C
                pool.wait_ge(m["scaled"], n + 1)
                pool.tensor_tensor(pair[:, :], prod[:, o:o + 2 * C], prod[:, o + 2 * C:o + 4 * C],
                                   ALU.add).then_inc(m["pair"], 1)
                pool.wait_ge(m["pair"], n + 1)
                pool.tensor_tensor(psum1[:, :], pair[:, 0:C], pair[:, C:2 * C], ALU.add).then_inc(m["psum1"], 1)
                pool.wait_ge(m["psum1"], n + 1)
                pool.wait_ge(m["combine"], HALF * (n + 1))
                pool.tensor_tensor(seq(DST[f], b, t * C, C), acc[:, (t % 2) * C:(t % 2 + 1) * C], psum1[:, :],
                                   ALU.add).then_inc(m["out"], 1)

            def moe_body(f, b):
                moe_rstd(f, b + 1)
                for t in range(TILES):
                    moe_sum(f, b, t)

            def moe_phase(f):
                moe_rstd(f, 0)
                moe_body(f, 0)
                with pool.Fori(1, BATCHES - 1) as b:
                    moe_body(f, b)
                for t in range(TILES):
                    moe_sum(f, BATCHES - 1, t)

            def att_rstd(b):
                inverse_root(rstd, vtmp, mv, 1.0 + EPS, EPS * EPS, a["meanvar"], a["var_eps"], a["rstd"], b, a["n2"], b)

            def att_rstd2(b):
                inverse_root(rstd2, vtmp2, mv2, 1.0, EPS, a["meanvar2"], a["var2_eps"], a["rstd2"], b, a["n1"], TILES * b)

            def att_e2v(b):
                pool.wait_ge(a["e12"], b + 1)
                pool.wait_ge(a["v_copied"], b + 1)
                pool.tensor_tensor(e12[:, TOK:2 * TOK], e12[:, 2 * TOK:3 * TOK], vS[:, :], ALU.mult).then_inc(a["e2v"], 1)

            def att_rstd3(b):
                inverse_root(rstd3, vtmp3, mv3, 1.0, EPS, a["meanvar3"], a["var3_eps"], a["rstd3"], b, a["n3"], TILES * b)

            def att_xs(b):
                pool.wait_ge(a["XR"], b + 1)
                wait_if(pool, a["out"], b)
                pool.tensor_tensor(xs[:, :], seq(X1, b), XR[:, :], ALU.add).then_inc(a["xs"], 1)

            def att_square(b, j):
                pool.wait_ge(a["relu"], HC * b + j + 1)
                wait_if(pool, a["kv"], b)
                o = (j % 2) * TOK
                pool.tensor_tensor(kf[:, j * TOK:(j + 1) * TOK], rl[:, o:o + TOK], rl[:, o:o + TOK],
                                   ALU.mult).then_inc(a["kf2"], 1)

            pool.memset(bexp[:, :], 0.0).then_inc(s_z, 1)
            pool.memset(mhalf[:, :], -0.5).then_inc(s_const, 1)
            pool.wait_ge(s_const, 1)
            moe_phase(0)
            att_rstd(0)
            att_rstd2(0)
            att_e2v(0)
            def att_body(b):
                att_rstd(b)
                att_rstd2(b)
                att_rstd3(b - 1)
                att_xs(b - 1)
                att_square(b - 1, 0)
                att_square(b - 1, 1)
                att_e2v(b)
                att_square(b - 1, 2)
                att_square(b - 1, 3)

            att_body(1)
            with pool.Fori(2, BATCHES) as b:
                att_body(b)
            att_rstd3(BATCHES - 1)
            att_xs(BATCHES - 1)
            for j in range(HC):
                att_square(BATCHES - 1, j)
            moe_phase(1)


def kernel(**inputs):
    import numpy as np
    import concourse.bacc as bacc
    from concourse.bass_utils import run_bass_kernel_spmd

    g = {k.replace("L0_attn_", "").replace("L0_ffn_", ""): np.asarray(v) for k, v in inputs.items()}
    cc = np.ascontiguousarray
    vectors = [g[n] for n in ("time_decay", "time_first", "tmk", "tmv", "tmr", "ln1_w", "ln1_b", "ln2_w", "ln2_b",
                              "cmk", "cmr")]
    arrays = {
        "x_in": cc(g["x"].reshape(BATCHES * TOK, C)),
        "vectors": cc(np.stack(vectors, axis=1)),
        "ln0_w": cc(g["ln0_w"]), "ln0_b": cc(g["ln0_b"]),
        "w_att": cc(np.concatenate([g[n].T for n in ("Wk", "Wv", "Wr", "Wo", "Wfr")], axis=1)),
        "w_ffn_k": cc(g["Wfk"].T),
        "w_ffn_v": cc(g["Wfv"].T.reshape(HC, C, C).transpose(1, 0, 2).reshape(C, HC * C)),
        "w_exp": cc(g["We"].transpose(1, 0, 2).reshape(C, E * C)),
        "b_exp": cc(g["be"]),
        "w_gate": cc(g["Wg"]),
        "b_gate": cc(np.broadcast_to(g["bg"], (C, TILES, E)).reshape(C, TILES * E)),
        "ident": np.eye(C, dtype=np.float32),
    }
    nc = bacc.Bacc("TRN2", target_bir_lowering=False, num_devices=1)
    args = [nc.dram_tensor(f"in_{n}", v.shape, mybir.dt.from_np(v.dtype), kind="ExternalInput").ap()
            for n, v in arrays.items()]
    out = nc.dram_tensor("y_out", (BATCHES * TOK, C), F32, kind="ExternalOutput").ap()
    macaron_kernel(nc, *args, out)
    r = run_bass_kernel_spmd(nc, [{f"in_{n}": v for n, v in arrays.items()}], core_ids=[0])
    return r.results[0]["y_out"].reshape(BATCHES, TOK, C)
```

```python
from contextlib import ExitStack

import concourse.bass as bass
from concourse import mybir

ALU = mybir.AluOpType
ACT = mybir.ActivationFunctionType
AX_X = mybir.AxisListType.X
F32 = mybir.dt.float32

C = 128
BATCHES = 4
TOK = 512
TILES = TOK // C
E = 8
HALF = E // 2
HC = 4
EPS = 1e-5
LOWEST = -1e38
NEVER = -3.4e38

V_DECAY, V_FIRST, V_TMK, V_TMV, V_TMR, V_LN1W, V_LN1B, V_LN2W, V_LN2B, V_CMK, V_CMR = range(11)
NV = 11


def macaron_kernel(nc, x, vectors, ln0_w, ln0_b, w_att, w_ffn_k, w_ffn_v, w_exp, b_exp, w_gate, b_gate, ident_in, out):
    with ExitStack() as ctx:
        def sb(name, *shape):
            return ctx.enter_context(nc.sbuf_tensor(name, list(shape), F32))

        def sem(name):
            return ctx.enter_context(nc.semaphore(name))

        X = sb("X", C, BATCHES * TOK)
        X1 = sb("X1", C, BATCHES * TOK)
        X0 = sb("X0", C, BATCHES * TOK)
        X2 = sb("X2", C, BATCHES * TOK)
        Y = sb("Y", C, BATCHES * TOK)
        ident = sb("ident", C, C)
        vec = sb("vec", C, NV)
        w0b = sb("w0b", C, C)
        b0b = sb("b0b", C, C)
        watt = sb("watt", C, 5 * C)
        wfk = sb("wfk", C, HC * C)
        wfv = sb("wfv", C, HC * C)
        wexp = sb("wexp", C, E * C)
        bexp = sb("bexp", TILES * E, TILES * C)
        wgate = sb("wgate", C, E)
        bgate = sb("bgate", C, TILES * E)
        mhalf = sb("mhalf", C, TILES)
        decay = sb("decay", C, 1)
        warm = sb("warm", C, 1)
        decay_w = sb("decay_w", C, TOK)
        stats = sb("stats", C, TILES * 6)
        mv = sb("mv", C, TILES * 2)
        statsA = sb("statsA", C, TILES * 6)
        mvA = sb("mvA", C, TILES * 2)
        rstds = [sb(f"rstds{f}", C, BATCHES * TILES) for f in range(3)]
        shifts = [sb(f"shifts{f}", C, BATCHES * TILES) for f in range(3)]
        vtmp = sb("vtmp", C, TILES)
        vtmpA = sb("vtmpA", C, TILES)
        negmeanA = sb("negmeanA", C, TILES)
        xn = sb("xn", C, TOK)
        xnT = sb("xnT", C, TOK)
        xnG = sb("xnG", C, TOK)
        negmean = sb("negmean", C, TILES)
        logit = sb("logit", C, TILES * E)
        top = sb("top", C, TILES * E)
        top2 = sb("top2", C, TILES * E)
        rest = sb("rest", C, TILES * E)
        shifted = sb("shifted", C, TILES * E)
        expo = sb("expo", C, TILES * E)
        chosen = sb("chosen", C, TILES * E)
        gsum = sb("gsum", C, TILES)
        ginv = sb("ginv", C, TILES)
        gate_next = sb("gate_next", C, TILES * E)
        gate = sb("gate", C, TILES * E)
        gateT = sb("gateT", TILES * E, C)
        base = sb("base", C, TOK)
        acc = sb("acc", C, 2 * C)
        prod = sb("prod", C, 2 * HALF * C)
        pair = sb("pair", C, 2 * C)
        psum1 = sb("psum1", C, C)
        n2 = sb("n2", C, TOK)
        t0 = sb("t0", C, TOK)
        stats2 = sb("stats2", C, TILES * 6)
        mv2 = sb("mv2", C, TILES * 2)
        stats3 = sb("stats3", C, TILES * 6)
        mv3 = sb("mv3", C, TILES * 2)
        rstd2 = sb("rstd2", C, TILES)
        vtmp2 = sb("vtmp2", C, TILES)
        rstd3 = sb("rstd3", C, TILES)
        vtmp3 = sb("vtmp3", C, TILES)
        negmean2 = sb("negmean2", C, TILES)
        shift2 = sb("shift2", C, TILES)
        negmean3 = sb("negmean3", C, TILES)
        shift3 = sb("shift3", C, TILES)
        n1 = sb("n1", C, TOK)
        h1 = sb("h1", C, TOK + 1)
        dh = sb("dh", C, TOK)
        xk = sb("xk", C, TOK)
        xv = sb("xv", C, TOK)
        xr = sb("xr", C, TOK)
        kS = sb("kS", C, TOK)
        vS = sb("vS", C, TOK)
        th = sb("th", C, TOK)
        PP = sb("PP", C, TOK + 1)
        q = sb("q", C, TOK)
        qq = sb("qq", C, 2 * TOK)
        de = sb("de", C, 2 * TOK)
        z = sb("z", C, TOK)
        zz = sb("zz", C, 2 * TOK)
        e12 = sb("e12", C, 3 * TOK)
        ev = sb("ev", C, TOK)
        AB = sb("AB", C, 2 * (TOK + 1))
        nd0 = sb("nd0", C, 2 * TOK)
        nd = sb("nd", C, 2 * TOK)
        rden = sb("rden", C, TOK)
        att = sb("att", C, TOK)
        sa = sb("sa", C, TOK)
        XR = sb("XR", C, TOK)
        xs = sb("xs", C, TOK)
        n3 = sb("n3", C, TOK)
        h2 = sb("h2", C, TOK + 1)
        dh2 = sb("dh2", C, TOK)
        xk2 = sb("xk2", C, TOK)
        xr2 = sb("xr2", C, TOK)
        rl = sb("rl", C, HC * TOK)
        kf = sb("kf", C, HC * TOK)
        th2 = sb("th2", C, TOK)
        rkv = sb("rkv", C, TOK)

        bank = [ctx.enter_context(nc.psum_tensor(f"bank{i}", [C, TOK], F32)) for i in range(8)]
        ps_exp = [bank[3], bank[5]], [bank[6], bank[7]]
        ps_xT, ps_gate, ps_base = bank[0], bank[1], bank[2]
        ps_k, ps_v, ps_r, ps_o = bank[0], bank[1], bank[2], bank[3]
        ps_hT, ps_h2T = bank[4], bank[7]
        ps_kf = [bank[5], bank[6]]
        ps_r2, ps_kv = bank[7], bank[4]

        s_x0 = sem("x_first_loaded")
        s_xr = sem("x_rest_loaded")
        s_id = sem("ident_loaded")
        s_wg = sem("gate_weights_loaded")
        s_we = sem("expert_weights_loaded")
        s_be = sem("expert_biases_loaded")
        s_vec = sem("vectors_loaded")
        s_wa = sem("attention_weights_loaded")
        s_z = sem("bias_block_zeroed")
        s_const = sem("pool_constants_set")
        s_pres = sem("dve_constants_set")
        s_warm = sem("table_warmer_set")
        s_dec = sem("decay_exponential")
        s_out = sem("output_stored")

        s_passed_dve = sem("dve_wait_passed")
        s_passed_pool = sem("pool_wait_passed")

        MOE = ("stats", "meanvar", "var_eps", "rstd", "shift", "norm", "xT", "xG", "xT_copied", "logits", "gate_step",
               "gate",
               "shifted", "exp", "gateT", "gateT_copied", "bias", "base", "exp_lo", "exp_hi", "combine",
               "scaled", "pair", "psum1", "out")
        ATT = ("stats", "meanvar", "var_eps", "rstd", "shift", "n2", "x0_step", "stats2", "meanvar2", "var2_eps", "rstd2",
               "shift2",
               "n1", "hT", "h1", "diff", "mixed", "k", "v", "r", "k_copied", "v_copied", "th",
               "qq", "de", "zz", "e12", "e2v", "wkv", "sa", "o", "XR", "stats3", "meanvar3", "var3_eps", "rstd3", "shift3",
               "n3", "h2T", "h2", "diff2", "mixed2", "kf", "relu", "kf2", "r2", "th2", "kv", "xs", "rkv", "out")
        moe = [{n: sem(f"moe{f}_{n}") for n in MOE} for f in range(2)]
        a = {n: sem(f"att_{n}") for n in ATT}

        SRC, DST = (X, X2), (X1, Y)
        G = 9
        W = 10

        def seq(t, b, lo=0, n=TOK):
            return t[:, bass.ds(b * TOK + lo, n)]

        def grp(ap, n):
            return ap.rearrange("p (t n) -> p t n", n=n)

        def wait_if(eng, s, v):
            if not isinstance(v, int) or v > 0:
                eng.wait_ge(s, v)

        block = ctx.enter_context(nc.Block())

        @block.sync
        def _(sp):
            xin = x.rearrange("(b t p) c -> p b t c", t=TILES, p=C)
            dst = X[:, :].rearrange("p (b t c) -> p b t c", b=BATCHES, t=TILES)
            sp.dma_start(dst[:, 0], xin[:, 0]).then_inc(s_x0, 16)
            sp.dma_start(wgate[:, :], w_gate).then_inc(s_wg, 16)
            sp.dma_start(bgate[:, :], b_gate).then_inc(s_wg, 16)
            for b in range(1, BATCHES):
                sp.dma_start(dst[:, b], xin[:, b]).then_inc(s_xr, 16)
            sp.dma_start(vec[:, :], vectors).then_inc(s_vec, 16)
            sp.dma_start(w0b[:, :], ln0_w.partition_broadcast(C)).then_inc(s_vec, 16)
            sp.dma_start(b0b[:, :], ln0_b.partition_broadcast(C)).then_inc(s_vec, 16)
            yout = out.rearrange("(b t p) c -> p b t c", t=TILES, p=C)
            ysb = Y[:, :].rearrange("p (b t c) -> p b t c", b=BATCHES, t=TILES)
            for b in range(BATCHES):
                sp.wait_ge(moe[1]["out"], TILES * (b + 1))
                sp.dma_start(yout[:, b], ysb[:, b]).then_inc(s_out, 16)
            sp.wait_ge(s_out, 16 * BATCHES)

        @block.tensor
        def _(pe):
            def moe_transposes(f, b):
                m = moe[f]
                pe.wait_ge(m["norm"], b + 1)
                for t in range(TILES):
                    mm = pe.transpose(ps_xT[:, t * C:(t + 1) * C], xn[:, t * C:(t + 1) * C], ident[:, :])
                mm.then_inc(m["xT"], 1)

            def moe_logits(f, b):
                m = moe[f]
                pe.wait_ge(m["xG"], b + 1)
                for t in range(TILES):
                    mm = pe.matmul(ps_gate[:, t * E:(t + 1) * E], xnG[:, t * C:(t + 1) * C], wgate[:, :],
                                   start=True, stop=True)
                mm.then_inc(m["logits"], 1)

            def moe_gateT(f, b):
                m = moe[f]
                pe.wait_ge(m["gate_step"], G * b + G)
                pe.transpose(ps_gate[0:TILES * E, C:2 * C], gate_next[:, :], ident[:, :]).then_inc(m["gateT"], 1)

            def moe_bias(f, b):
                m = moe[f]
                pe.wait_ge(m["gateT_copied"], b + 1)
                pe.matmul(ps_base[:, :], gateT[:, :], bexp[:, :], start=True, stop=True).then_inc(m["bias"], 1)

            def moe_experts(f, b, t):
                m = moe[f]
                n = TILES * b + t
                pe.wait_ge(m["xT_copied"], n + 1)
                for half, (done, freed, per) in enumerate(((m["exp_lo"], m["combine"], HALF), (m["exp_hi"], m["scaled"], 1))):
                    if not isinstance(b, int) or n >= 2:
                        pe.wait_ge(freed, (n - 1) * per)
                    pe.matmul(ps_exp[half][t % 2][:, :], xnT[:, t * C:(t + 1) * C],
                              wexp[:, half * HALF * C:(half + 1) * HALF * C], start=True, stop=True).then_inc(done, 1)

            def moe_tile(f, b, t, last=False):
                moe_experts(f, b, t)
                if t == 0 and not last:
                    moe_transposes(f, b + 1)
                if t == 0:
                    moe_bias(f, b)
                if t == 1 and not last:
                    moe_logits(f, b + 1)
                if t == 3 and not last:
                    moe_gateT(f, b + 1)

            def moe_body(f, b, last=False):
                for t in range(TILES):
                    moe_tile(f, b, t, last)

            def att_transpose(b):
                pe.wait_ge(a["n1"], b + 1)
                for t in range(TILES):
                    mm = pe.transpose(ps_hT[:, t * C:(t + 1) * C], n1[:, t * C:(t + 1) * C], ident[:, :])
                mm.then_inc(a["hT"], 1)

            def att_kvr(b):
                for i, (ps, src, done, freed) in enumerate(((ps_k, xk, a["k"], a["k_copied"]), (ps_v, xv, a["v"], a["v_copied"]),
                                                            (ps_r, xr, a["r"], a["th"]))):
                    wait_if(pe, freed, b)
                    pe.wait_ge(a["mixed"], 3 * b + i + 1)
                    pe.matmul(ps[:, :], watt[:, i * C:(i + 1) * C], src[:, :], start=True, stop=True).then_inc(done, 1)

            def att_o(b):
                pe.wait_ge(a["sa"], b + 1)
                for t in range(TILES):
                    mm = pe.matmul(ps_o[:, t * C:(t + 1) * C], sa[:, t * C:(t + 1) * C], watt[:, 3 * C:4 * C],
                                   start=True, stop=True)
                mm.then_inc(a["o"], 1)

            def att_transpose2(b):
                pe.wait_ge(a["n3"], b + 1)
                for t in range(TILES):
                    mm = pe.transpose(ps_h2T[:, t * C:(t + 1) * C], n3[:, t * C:(t + 1) * C], ident[:, :])
                mm.then_inc(a["h2T"], 1)

            def att_kf(b):
                for j in range(HC):
                    if j >= 2:
                        pe.wait_ge(a["relu"], HC * b + j - 1)
                    if j == 0:
                        pe.wait_ge(a["mixed2"], 2 * b + 1)
                    pe.matmul(ps_kf[j % 2][:, :], wfk[:, j * C:(j + 1) * C], xk2[:, :],
                              start=True, stop=True).then_inc(a["kf"], 1)

            def att_r2(b):
                pe.wait_ge(a["mixed2"], 2 * b + 2)
                pe.wait_ge(a["h2"], b + 1)
                for t in range(TILES):
                    mm = pe.matmul(ps_r2[:, t * C:(t + 1) * C], xr2[:, t * C:(t + 1) * C], watt[:, 4 * C:5 * C],
                                   start=True, stop=True)
                mm.then_inc(a["r2"], 1)

            def att_kv(b):
                pe.wait_ge(a["kf2"], HC * b + HC)
                for t in range(TILES):
                    for j in range(HC):
                        mm = pe.matmul(ps_kv[:, t * C:(t + 1) * C], kf[:, j * TOK + t * C:j * TOK + (t + 1) * C],
                                       wfv[:, j * C:(j + 1) * C], start=(j == 0), stop=(j == HC - 1))
                mm.then_inc(a["kv"], 1)

            def att_body(b, front=True, rest=True):
                if rest:
                    att_o(b - 1)
                    att_transpose2(b - 1)
                if front:
                    att_transpose(b + 1)
                if rest:
                    att_kf(b - 1)
                    att_r2(b - 1)
                if front:
                    att_kvr(b + 1)
                if rest:
                    att_kv(b - 1)

            pe.wait_ge(s_id, 16)
            moe_transposes(0, 0)
            pe.wait_ge(s_wg, 32)
            moe_logits(0, 0)
            moe_gateT(0, 0)
            pe.wait_ge(s_we, 16)
            pe.wait_ge(s_be, 16 * TILES)
            moe_body(0, 0)
            with pe.Fori(1, BATCHES - 1) as b:
                moe_body(0, b)
            pe.wait_ge(s_wa, 48)
            last = BATCHES - 1
            moe_tile(0, last, 0, True)
            moe_tile(0, last, 1, True)
            moe_tile(0, last, 2, True)
            att_transpose(0)
            moe_tile(0, last, 3, True)
            pe.wait_ge(moe[0]["base"], BATCHES)
            att_kvr(0)
            pe.wait_ge(moe[0]["combine"], HALF * TILES * BATCHES)
            pe.wait_ge(moe[0]["scaled"], TILES * BATCHES)

            att_body(0, rest=False)
            with pe.Fori(1, BATCHES - 1) as b:
                att_body(b)
            att_body(BATCHES - 1, front=False)

            att_o(last)
            pe.wait_ge(a["th"], BATCHES)
            moe_transposes(1, 0)
            att_transpose2(last)
            moe_logits(1, 0)
            att_kf(last)
            att_r2(last)
            moe_gateT(1, 0)
            pe.wait_ge(a["relu"], HC * BATCHES)
            pe.wait_ge(a["th2"], BATCHES)
            moe_tile(1, 0, 0)
            moe_tile(1, 0, 1)
            att_kv(last)
            moe_tile(1, 0, 2)
            moe_tile(1, 0, 3)
            with pe.Fori(1, BATCHES - 1) as b:
                moe_body(1, b)
            moe_body(1, BATCHES - 1, True)

        @block.vector
        def _(dve):
            def settled():
                dve.sem_inc(s_passed_dve, 1)

            def layer_stats(src, st, out2, s_stats, s_mv, b, s_free=None):
                settled()
                if s_free is not None:
                    wait_if(dve, s_mv, b)
                    settled()
                for t in range(TILES):
                    i = dve.bn_stats(st[:, t * 6:(t + 1) * 6], src(t))
                i.then_inc(s_stats, 1)
                if s_free is not None:
                    wait_if(dve, s_free, b)
                    settled()
                dve.wait_ge(s_stats, b + 1)
                settled()
                for t in range(TILES):
                    i = dve.bn_aggr(out2[:, t * 2:(t + 1) * 2], st[:, t * 6:(t + 1) * 6])
                i.then_inc(s_mv, 1)

            def moe_stats(f, b):
                m = moe[f]
                if f == 0:
                    if isinstance(b, int):
                        dve.wait_ge(s_x0, 16)
                    else:
                        dve.wait_ge(s_xr, 16 * (BATCHES - 1))
                else:
                    dve.wait_ge(a["out"], b + 1)
                layer_stats(lambda t: seq(SRC[f], b, t * C, C), stats, mv, m["stats"], m["meanvar"], b,
                            m["var_eps"] if f == 0 else None)

            def moe_gates(f, b, k):
                m = moe[f]

                def step(i):
                    i.then_inc(m["gate_step"], 1)
                if k:
                    dve.wait_ge(m["gate_step"], G * b + k)
                if k == 0:
                    if f == 0:
                        dve.wait_ge(s_wg, 32)
                    dve.wait_ge(m["logits"], b + 1)
                    step(dve.tensor_tensor(logit[:, :], ps_gate[:, 0:TILES * E], bgate[:, :], ALU.add))
                elif k == 1:
                    settled()
                    for t in range(TILES):
                        i = dve.max(top[:, t * E:(t + 1) * E], logit[:, t * E:(t + 1) * E])
                    step(i)
                elif k == 2:
                    dve.tensor_tensor(grp(shifted[:, :], E), grp(logit[:, :], E),
                                      grp(top[:, :], E)[:, :, 0:1].to_broadcast([C, TILES, E]),
                                      ALU.subtract).then_inc(m["shifted"], 1)
                    step(dve.tensor_copy(grp(top2[:, :], E)[:, :, 0:2], grp(top[:, :], E)[:, :, 0:2]))
                elif k == 3:
                    settled()
                    for t in range(TILES):
                        s = slice(t * E, (t + 1) * E)
                        i = dve.match_replace(rest[:, s], top2[:, s], logit[:, s], NEVER)
                    step(i)
                elif k == 4:
                    step(dve.tensor_tensor(chosen[:, :], logit[:, :], rest[:, :], ALU.not_equal))
                elif k == 5:
                    dve.wait_ge(m["exp"], b + 1)
                    step(dve.tensor_tensor(chosen[:, :], expo[:, :], chosen[:, :], ALU.mult))
                elif k == 6:
                    step(dve.tensor_reduce(gsum[:, :], grp(chosen[:, :], E), AX_X, ALU.add))
                elif k == 7:
                    step(dve.reciprocal(ginv[:, :], gsum[:, :]))
                else:
                    step(dve.scalar_tensor_tensor(grp(gate_next[:, :], E), grp(chosen[:, :], E), 0.5,
                                                  ginv[:, :].unsqueeze(2).to_broadcast([C, TILES, E]),
                                                  ALU.mult, ALU.mult))

            def moe_base(f, b):
                m = moe[f]
                dve.wait_ge(m["gate_step"], G * b + G)
                wait_if(dve, m["scaled"], TILES * b)
                wait_if(dve, m["combine"], HALF * TILES * b)
                dve.tensor_copy(gate[:, :], gate_next[:, :]).then_inc(m["gate"], 1)
                dve.wait_ge(m["bias"], b + 1)
                dve.tensor_tensor(base[:, :], ps_base[:, :], seq(SRC[f], b), ALU.add).then_inc(m["base"], 1)
                dve.wait_ge(m["gate"], b + 1)
                dve.wait_ge(m["base"], b + 1)

            def moe_combine(f, b, t, e):
                m = moe[f]
                n = TILES * b + t
                half = acc[:, (t % 2) * C:(t % 2 + 1) * C]
                if e:
                    dve.wait_ge(m["combine"], HALF * n + e)
                else:
                    dve.wait_ge(m["exp_lo"], n + 1)
                    if not isinstance(b, int) or n >= 2:
                        dve.wait_ge(m["out"], n - 1)
                dve.scalar_tensor_tensor(half, ps_exp[0][t % 2][:, e * C:(e + 1) * C],
                                         gate[:, t * E + e:t * E + e + 1],
                                         base[:, t * C:(t + 1) * C] if e == 0 else half,
                                         ALU.mult, ALU.add).then_inc(m["combine"], 1)

            def moe_tile(f, b, t, last=False):
                if t == 0:
                    moe_base(f, b)
                for e in range(HALF):
                    moe_combine(f, b, t, e)
                    k = (t - 1) * HALF + e
                    if 0 <= k < G and not last:
                        moe_gates(f, b + 1, k)

            def moe_body(f, b, last=False):
                for t in range(TILES):
                    moe_tile(f, b, t, last)

            def att_stats(b):
                dve.wait_ge(moe[0]["out"], TILES * (b + 1))
                layer_stats(lambda t: seq(X1, b, t * C, C), statsA, mvA, a["stats"], a["meanvar"], b)

            def att_stats2(b):
                dve.wait_ge(a["x0_step"], 2 * b + 2)
                layer_stats(lambda t: seq(X0, b, t * C, C), stats2, mv2, a["stats2"], a["meanvar2"], b)

            def att_mix(b):
                dve.wait_ge(a["h1"], b + 1)
                dve.tensor_tensor(dh[:, :], h1[:, 1:TOK + 1], h1[:, 0:TOK], ALU.subtract).then_inc(a["diff"], 1)
                dve.wait_ge(a["diff"], b + 1)
                for dst, col, used in ((xk, V_TMK, a["k"]), (xv, V_TMV, a["v"]), (xr, V_TMR, a["r"])):
                    wait_if(dve, used, b)
                    dve.scalar_tensor_tensor(dst[:, :], dh[:, :], vec[:, col:col + 1], h1[:, 0:TOK],
                                             ALU.mult, ALU.add).then_inc(a["mixed"], 1)

            def wkv_step(b, k):
                dve.wait_ge(a["wkv"], W * b + k)

            def wkv_done(i):
                i.then_inc(a["wkv"], 1)
            lo, hi = slice(0, TOK), slice(TOK, 2 * TOK)

            def wkv_exponents(b):
                dve.wait_ge(a["k_copied"], b + 1)
                wkv_done(dve.tensor_tensor_scan(PP[:, 1:TOK + 1], decay_w[:, :], kS[:, :], LOWEST, ALU.add, ALU.max))
                wkv_step(b, 1)
                wkv_done(dve.scalar_tensor_tensor(q[:, :], PP[:, 0:TOK], decay[:, 0:1], kS[:, :],
                                                  ALU.add, ALU.subtract))
                wkv_done(dve.scalar_tensor_tensor(z[:, :], kS[:, :], vec[:, V_FIRST:V_FIRST + 1], PP[:, 0:TOK],
                                                  ALU.add, ALU.subtract))

            def wkv_scans(b):
                dve.wait_ge(a["de"], b + 1)
                dve.wait_ge(a["v_copied"], b + 1)
                wkv_done(dve.tensor_tensor(ev[:, :], de[:, hi], vS[:, :], ALU.mult))
                wkv_done(dve.tensor_tensor_scan(AB[:, TOK + 2:2 * TOK + 2], de[:, lo], de[:, hi], 0.0,
                                                ALU.mult, ALU.add))
                wkv_step(b, 4)
                wkv_done(dve.tensor_tensor_scan(AB[:, 1:TOK + 1], de[:, lo], ev[:, :], 0.0, ALU.mult, ALU.add))

            def wkv_old(b):
                wkv_step(b, 6)
                dve.wait_ge(a["e12"], b + 1)
                ab = AB[:, :].rearrange("p (s n) -> p s n", s=2)[:, :, 0:TOK]
                wkv_done(dve.tensor_tensor(grp(nd0[:, :], TOK), ab, e12[:, lo].unsqueeze(1).to_broadcast([C, 2, TOK]),
                                           ALU.mult))

            def wkv_new(b):
                wkv_step(b, 7)
                dve.wait_ge(a["e2v"], b + 1)
                wkv_done(dve.tensor_tensor(nd[:, :], nd0[:, :], e12[:, TOK:3 * TOK], ALU.add))

            def wkv_divide(b):
                wkv_step(b, 8)
                wkv_done(dve.reciprocal(rden[:, :], nd[:, hi]))

            def wkv_out(b):
                wkv_step(b, 9)
                wkv_done(dve.tensor_tensor(att[:, :], nd[:, lo], rden[:, :], ALU.mult))
                wkv_step(b, 10)
                dve.wait_ge(a["th"], b + 1)
                dve.scalar_tensor_tensor(sa[:, :], th[:, :], 1.0, att[:, :], ALU.add, ALU.mult).then_inc(a["sa"], 1)

            def att_resid(b):
                dve.wait_ge(a["o"], b + 1)
                dve.scalar_tensor_tensor(XR[:, :], ps_o[:, :], 0.5, seq(X0, b), ALU.mult, ALU.add).then_inc(a["XR"], 1)
                dve.wait_ge(a["XR"], b + 1)

                def src(t):
                    return XR[:, t * C:(t + 1) * C]
                layer_stats(src, stats3, mv3, a["stats3"], a["meanvar3"], b)

            def att_mix2(b):
                dve.wait_ge(a["h2"], b + 1)
                dve.tensor_tensor(dh2[:, :], h2[:, 1:TOK + 1], h2[:, 0:TOK], ALU.subtract).then_inc(a["diff2"], 1)
                dve.wait_ge(a["diff2"], b + 1)
                dve.scalar_tensor_tensor(xk2[:, :], dh2[:, :], vec[:, V_CMK:V_CMK + 1], h2[:, 0:TOK],
                                         ALU.mult, ALU.add).then_inc(a["mixed2"], 1)
                dve.scalar_tensor_tensor(xr2[:, :], dh2[:, :], vec[:, V_CMR:V_CMR + 1], h2[:, 0:TOK],
                                         ALU.mult, ALU.add).then_inc(a["mixed2"], 1)

            def att_out(b):
                dve.wait_ge(a["kv"], b + 1)
                dve.wait_ge(a["th2"], b + 1)
                dve.scalar_tensor_tensor(rkv[:, :], th2[:, :], 1.0, ps_kv[:, :], ALU.add, ALU.mult).then_inc(a["rkv"], 1)
                dve.wait_ge(a["rkv"], b + 1)
                dve.wait_ge(a["xs"], b + 1)
                dve.scalar_tensor_tensor(seq(X2, b), rkv[:, :], 0.5, xs[:, :], ALU.mult, ALU.add).then_inc(a["out"], 1)

            dve.memset(warm[:, :], 0.0).then_inc(s_warm, 1)
            for t, v in ((top2[:, :], NEVER), (h1[:, 0:1], 0.0), (h2[:, 0:1], 0.0), (PP[:, 0:1], LOWEST),
                         (AB[:, 0:1], 0.0), (AB[:, TOK + 1:TOK + 2], 0.0)):
                dve.memset(t, v).then_inc(s_pres, 1)
            dve.memset(decay_w[:, :], 0.0).then_inc(s_pres, 1)
            dve.wait_ge(s_pres, 7)
            moe_stats(0, 0)
            with dve.Fori(1, BATCHES) as b:
                moe_stats(0, b)
            dve.wait_ge(s_vec, 48)
            dve.wait_ge(s_dec, 1)
            dve.tensor_scalar(decay[:, :], decay[:, :], -1.0, None, ALU.mult).then_inc(s_dec, 1)
            dve.wait_ge(s_dec, 2)
            dve.tensor_scalar(decay_w[:, :], decay_w[:, :], decay[:, 0:1], None, ALU.add).then_inc(s_dec, 1)
            dve.wait_ge(s_dec, 3)
            for k in range(G):
                moe_gates(0, 0, k)
            moe_body(0, 0)
            with dve.Fori(1, BATCHES - 1) as b:
                moe_tile(0, b, 0)
                att_stats(b - 1)
                moe_tile(0, b, 1)
                moe_tile(0, b, 2)
                moe_tile(0, b, 3)
            last = BATCHES - 1
            moe_tile(0, last, 0, True)
            att_stats(last - 1)
            moe_tile(0, last, 1, True)
            att_stats2(0)
            moe_tile(0, last, 2, True)
            moe_tile(0, last, 3, True)
            att_mix(0)
            att_stats(last)

            def att_body(b, front=True, wkv=True, rest=True):
                if wkv:
                    wkv_exponents(b)
                if rest:
                    att_resid(b - 1)
                if front:
                    att_stats2(b + 1)
                if wkv:
                    wkv_scans(b)
                    wkv_old(b)
                if rest:
                    att_mix2(b - 1)
                if wkv:
                    wkv_new(b)
                if front:
                    att_mix(b + 1)
                if wkv:
                    wkv_divide(b)
                    wkv_out(b)
                if rest:
                    att_out(b - 1)
                    moe_stats(1, b - 1)

            att_body(0, rest=False)
            with dve.Fori(1, BATCHES - 1) as b:
                att_body(b)
            att_body(BATCHES - 1, front=False)

            att_resid(last)
            att_mix2(last)
            for k in range(G):
                moe_gates(1, 0, k)
            moe_tile(1, 0, 0)
            moe_tile(1, 0, 1)
            att_out(last)
            moe_stats(1, last)
            moe_tile(1, 0, 2)
            moe_tile(1, 0, 3)
            with dve.Fori(1, BATCHES - 1) as b:
                moe_body(1, b)
            moe_body(1, last, True)

        @block.scalar
        def _(act):
            def normalise(dst, src, rs, sh, s_shift, s_done, b):
                act.wait_ge(s_shift, b + 1)
                for t in range(TILES):
                    i = act.activation(dst[:, t * C:(t + 1) * C], src(t), ACT.Identity, bias=sh(t), scale=rs(t))
                i.then_inc(s_done, 1)

            def one(t, b):
                return lambda i: t[:, bass.ds(b * TILES + i, 1)]

            def moe_norm(f, b):
                m = moe[f]
                wait_if(act, m["xT"], b)
                normalise(xn, lambda t: seq(SRC[f], b, t * C, C), one(rstds[f], b), one(shifts[f], b), m["shift"],
                          m["norm"], b)

            def moe_copy_xG(f, b):
                m = moe[f]
                act.wait_ge(m["xT"], b + 1)
                act.copy(xnG[:, :], ps_xT[:, :]).then_inc(m["xG"], 1)

            def moe_copy_xT(f, b, t):
                m = moe[f]
                if not isinstance(b, int) or b > 0:
                    act.wait_ge(m["exp_hi"], TILES * (b - 1) + t + 1)
                act.copy(xnT[:, t * C:(t + 1) * C], ps_xT[:, t * C:(t + 1) * C]).then_inc(m["xT_copied"], 1)

            def moe_exp(f, b):
                m = moe[f]
                act.wait_ge(m["shifted"], b + 1)
                act.activation(expo[:, :], shifted[:, :], ACT.Exp).then_inc(m["exp"], 1)

            def moe_copy_gateT(f, b):
                m = moe[f]
                act.wait_ge(m["gateT"], b + 1)
                wait_if(act, m["bias"], b)
                act.copy(gateT[:, :], ps_gate[0:TILES * E, C:2 * C]).then_inc(m["gateT_copied"], 1)

            def moe_scale(f, b, t):
                m = moe[f]
                n = TILES * b + t
                if t == 0:
                    act.wait_ge(m["gate"], b + 1)
                act.wait_ge(m["exp_hi"], n + 1)
                if not isinstance(b, int) or n >= 2:
                    act.wait_ge(m["pair"], n - 1)
                for e in range(HALF):
                    o = ((t % 2) * HALF + e) * C
                    i = act.activation(prod[:, o:o + C], ps_exp[1][t % 2][:, e * C:(e + 1) * C], ACT.Copy,
                                       scale=gate[:, t * E + HALF + e:t * E + HALF + e + 1])
                i.then_inc(m["scaled"], 1)

            def moe_tile(f, b, t, last=False):
                if t == 0 and not last:
                    moe_norm(f, b + 1)
                moe_scale(f, b, t)
                if last:
                    return
                if t == 0:
                    moe_copy_xG(f, b + 1)
                if t == 1:
                    moe_exp(f, b + 1)
                moe_copy_xT(f, b + 1, t)
                if t == 3:
                    moe_copy_gateT(f, b + 1)

            def moe_body(f, b, last=False):
                for t in range(TILES):
                    moe_tile(f, b, t, last)

            def att_h1(b):
                act.wait_ge(a["hT"], b + 1)
                wait_if(act, a["mixed"], 3 * b)
                act.activation(h1[:, 1:TOK + 1], ps_hT[:, :], ACT.Identity, bias=vec[:, V_LN1B:V_LN1B + 1],
                               scale=vec[:, V_LN1W:V_LN1W + 1]).then_inc(a["h1"], 1)

            def att_kvr(b):
                act.wait_ge(a["k"], b + 1)
                wait_if(act, a["sa"], b)
                act.copy(kS[:, :], ps_k[:, :]).then_inc(a["k_copied"], 1)
                act.wait_ge(a["v"], b + 1)
                act.copy(vS[:, :], ps_v[:, :]).then_inc(a["v_copied"], 1)
                act.wait_ge(a["r"], b + 1)
                act.activation(th[:, :], ps_r[:, :], ACT.Tanh, scale=0.5).then_inc(a["th"], 1)

            def att_exps(b):
                for n, src, pos, neg, buf, s_relu in ((2, q, 1, 0, qq, a["qq"]), (3, z, 0, 1, zz, a["zz"])):
                    act.wait_ge(a["wkv"], W * b + n)
                    act.activation(buf[:, pos * TOK:(pos + 1) * TOK], src[:, :], ACT.Relu)
                    act.activation(buf[:, neg * TOK:(neg + 1) * TOK], src[:, :], ACT.Relu,
                                   scale=-1.0).then_inc(s_relu, 1)
                act.wait_ge(a["qq"], b + 1)
                act.activation(de[:, :], qq[:, :], ACT.Exp, scale=-1.0).then_inc(a["de"], 1)
                act.wait_ge(a["zz"], b + 1)
                act.activation(e12[:, :].rearrange("p (s n) -> p s n", s=3)[:, 0:3:2, :], grp(zz[:, :], TOK),
                               ACT.Exp, scale=-1.0).then_inc(a["e12"], 1)

            def att_h2(b):
                act.wait_ge(a["h2T"], b + 1)
                act.activation(h2[:, 1:TOK + 1], ps_h2T[:, :], ACT.Identity, bias=vec[:, V_LN2B:V_LN2B + 1],
                               scale=vec[:, V_LN2W:V_LN2W + 1]).then_inc(a["h2"], 1)

            def att_kf2(b):
                for j in range(0, HC, 2):
                    for i in range(2):
                        act.wait_ge(a["kf"], HC * b + j + i + 1)
                        act.activation(rl[:, (j + i) * TOK:(j + i + 1) * TOK], ps_kf[i][:, :], ACT.Relu).then_inc(a["relu"], 1)
                    for i in range(2):
                        act.wait_ge(a["relu"], HC * b + j + i + 1)
                        act.activation(kf[:, (j + i) * TOK:(j + i + 1) * TOK], rl[:, (j + i) * TOK:(j + i + 1) * TOK],
                                       ACT.Square).then_inc(a["kf2"], 1)

            def att_th2(b):
                act.wait_ge(a["r2"], b + 1)
                act.activation(th2[:, :], ps_r2[:, :], ACT.Tanh, scale=0.5).then_inc(a["th2"], 1)

            act.wait_ge(s_warm, 1)
            act.activation(expo[:, 0:1], warm[:, :], ACT.Exp)
            act.dma_start(ident[:, :], ident_in).then_inc(s_id, 16)
            act.dma_start(wexp[:, :], w_exp).then_inc(s_we, 16)
            act.wait_ge(s_z, 1)
            for t in range(TILES):
                act.dma_start(bexp[t * E:(t + 1) * E, t * C:(t + 1) * C], b_exp).then_inc(s_be, 16)
            act.dma_start(watt[:, :], w_att).then_inc(s_wa, 16)
            act.dma_start(wfk[:, :], w_ffn_k).then_inc(s_wa, 16)
            act.dma_start(wfv[:, :], w_ffn_v).then_inc(s_wa, 16)
            def att_n2(b):
                normalise(n2, lambda t: seq(X1, b, t * C, C), one(rstds[2], b), one(shifts[2], b), a["shift"], a["n2"], b)

            def att_n1(b):
                normalise(n1, lambda t: seq(X0, b, t * C, C), lambda t: rstd2[:, t:t + 1], lambda t: shift2[:, t:t + 1],
                          a["shift2"], a["n1"], b)

            def att_n3(b):
                normalise(n3, lambda t: XR[:, t * C:(t + 1) * C], lambda t: rstd3[:, t:t + 1],
                          lambda t: shift3[:, t:t + 1], a["shift3"], a["n3"], b)

            def att_body(b, front=True, rest=True):
                if front:
                    att_n2(b + 1)
                att_exps(b)
                if rest:
                    att_n3(b - 1)
                    att_h2(b - 1)
                if front:
                    att_n1(b + 1)
                    att_h1(b + 1)
                if rest:
                    att_kf2(b - 1)
                    att_th2(b - 1)
                if front:
                    att_kvr(b + 1)

            act.wait_ge(s_vec, 48)
            act.activation(decay[:, :], vec[:, V_DECAY:V_DECAY + 1], ACT.Exp).then_inc(s_dec, 1)
            act.wait_ge(s_pres, 7)
            act.wait_ge(s_x0, 16)
            moe_norm(0, 0)
            moe_copy_xG(0, 0)
            for t in range(TILES):
                moe_copy_xT(0, 0, t)
            moe_exp(0, 0)
            moe_copy_gateT(0, 0)
            act.wait_ge(s_xr, 16 * (BATCHES - 1))
            moe_body(0, 0)
            with act.Fori(1, BATCHES - 1) as b:
                moe_body(0, b)
            last = BATCHES - 1
            att_n2(0)
            moe_tile(0, last, 0, True)
            moe_tile(0, last, 1, True)
            att_n1(0)
            moe_tile(0, last, 2, True)
            moe_tile(0, last, 3, True)
            att_h1(0)
            att_kvr(0)

            att_body(0, rest=False)
            with act.Fori(1, BATCHES - 1) as b:
                att_body(b)
            att_body(last, front=False)

            moe_norm(1, 0)
            att_n3(last)
            moe_copy_xG(1, 0)
            for t in range(TILES):
                moe_copy_xT(1, 0, t)
            att_h2(last)
            moe_exp(1, 0)
            att_kf2(last)
            att_th2(last)
            moe_copy_gateT(1, 0)
            moe_body(1, 0)
            with act.Fori(1, BATCHES - 1) as b:
                moe_body(1, b)
            moe_body(1, last, True)

        @block.gpsimd
        def _(pool):
            def inverse_root(rs, tmp, neg, sh, out2, scale, add, s_mv, s_tmp, s_rs, s_shift, b, again=False):
                if again:
                    wait_if(pool, s_shift, b)
                    pool.sem_inc(s_passed_pool, 1)
                pool.wait_ge(s_mv, b + 1)
                pool.sem_inc(s_passed_pool, 1)
                pool.tensor_scalar(tmp[:, :], grp(out2[:, :], 2)[:, :, 1], scale, add, ALU.mult, ALU.add)
                pool.tensor_scalar(neg[:, :], grp(out2[:, :], 2)[:, :, 0], -1.0, None, ALU.mult).then_inc(s_tmp, 1)
                pool.wait_ge(s_tmp, b + 1)
                pool.tensor_tensor(rs, tmp[:, :], mhalf[:, :], ALU.pow).then_inc(s_rs, 1)
                pool.wait_ge(s_rs, b + 1)
                pool.tensor_tensor(sh, neg[:, :], rs, ALU.mult).then_inc(s_shift, 1)

            def four(t, b):
                return t[:, bass.ds(b * TILES, TILES)]

            def moe_rstd(f, b):
                m = moe[f]
                inverse_root(four(rstds[f], b), vtmp, negmean, four(shifts[f], b), mv, 1.0, EPS, m["meanvar"],
                             m["var_eps"], m["rstd"], m["shift"], b, f == 0)

            def moe_sum(f, b, t):
                m = moe[f]
                n = TILES * b + t
                o = (t % 2) * HALF * C
                pool.wait_ge(m["scaled"], n + 1)
                pool.tensor_tensor(pair[:, :], prod[:, o:o + 2 * C], prod[:, o + 2 * C:o + 4 * C],
                                   ALU.add).then_inc(m["pair"], 1)
                pool.wait_ge(m["pair"], n + 1)
                pool.tensor_tensor(psum1[:, :], pair[:, 0:C], pair[:, C:2 * C], ALU.add).then_inc(m["psum1"], 1)
                pool.wait_ge(m["psum1"], n + 1)
                pool.wait_ge(m["combine"], HALF * (n + 1))
                pool.tensor_tensor(seq(DST[f], b, t * C, C), acc[:, (t % 2) * C:(t % 2 + 1) * C], psum1[:, :],
                                   ALU.add).then_inc(m["out"], 1)

            def moe_body(f, b):
                for t in range(TILES):
                    moe_sum(f, b, t)

            def att_rstd(b):
                inverse_root(four(rstds[2], b), vtmpA, negmeanA, four(shifts[2], b), mvA, 1.0 + EPS, EPS * EPS, a["meanvar"], a["var_eps"],
                             a["rstd"], a["shift"], b)

            def att_rstd2(b):
                inverse_root(rstd2[:, :], vtmp2, negmean2, shift2[:, :], mv2, 1.0, EPS, a["meanvar2"], a["var2_eps"], a["rstd2"],
                             a["shift2"], b)

            def att_x0(b):
                pool.wait_ge(a["n2"], b + 1)
                pool.tensor_tensor(grp(t0[:, :], C), grp(n2[:, :], C),
                                   w0b[:, :].unsqueeze(1).to_broadcast([C, TILES, C]), ALU.mult).then_inc(a["x0_step"], 1)
                pool.wait_ge(a["x0_step"], 2 * b + 1)
                pool.tensor_tensor(grp(seq(X0, b), C), grp(t0[:, :], C),
                                   b0b[:, :].unsqueeze(1).to_broadcast([C, TILES, C]), ALU.add).then_inc(a["x0_step"], 1)

            def att_e2v(b):
                pool.wait_ge(a["e12"], b + 1)
                pool.wait_ge(a["v_copied"], b + 1)
                pool.tensor_tensor(e12[:, TOK:2 * TOK], e12[:, 2 * TOK:3 * TOK], vS[:, :], ALU.mult).then_inc(a["e2v"], 1)

            def att_rstd3(b):
                inverse_root(rstd3[:, :], vtmp3, negmean3, shift3[:, :], mv3, 1.0, EPS, a["meanvar3"], a["var3_eps"], a["rstd3"],
                             a["shift3"], b)

            def att_xs(b):
                pool.wait_ge(a["XR"], b + 1)
                pool.tensor_tensor(xs[:, :], seq(X1, b), XR[:, :], ALU.add).then_inc(a["xs"], 1)

            pool.memset(bexp[:, :], 0.0).then_inc(s_z, 1)
            pool.memset(mhalf[:, :], -0.5).then_inc(s_const, 1)
            pool.wait_ge(s_const, 1)
            moe_rstd(0, 0)
            with pool.Fori(1, BATCHES) as b:
                moe_rstd(0, b)
            moe_body(0, 0)
            with pool.Fori(1, BATCHES - 1) as b:
                moe_sum(0, b, 0)
                moe_sum(0, b, 1)
                att_rstd(b - 1)
                moe_sum(0, b, 2)
                moe_sum(0, b, 3)
            pool.wait_ge(s_vec, 48)
            last = BATCHES - 1
            att_x0(0)
            moe_sum(0, last, 0)
            att_rstd(last - 1)
            moe_sum(0, last, 1)
            att_rstd2(0)
            moe_sum(0, last, 2)
            moe_sum(0, last, 3)
            att_rstd(last)

            def att_body(b, front=True, wkv=True, rest=True):
                if front:
                    att_x0(b + 1)
                if rest:
                    att_rstd3(b - 1)
                if wkv:
                    att_e2v(b)
                if front:
                    att_rstd2(b + 1)
                if rest:
                    att_xs(b - 1)
                    moe_rstd(1, b - 1)

            att_body(0, rest=False)
            with pool.Fori(1, BATCHES - 1) as b:
                att_body(b)
            att_body(last, front=False)

            att_rstd3(last)
            att_xs(last)
            moe_sum(1, 0, 0)
            moe_sum(1, 0, 1)
            moe_rstd(1, last)
            moe_sum(1, 0, 2)
            moe_sum(1, 0, 3)
            with pool.Fori(1, BATCHES - 1) as b:
                moe_body(1, b)
            moe_body(1, last)


def kernel(**inputs):
    import numpy as np
    import concourse.bacc as bacc
    from concourse.bass_utils import run_bass_kernel_spmd

    g = {k.replace("L0_attn_", "").replace("L0_ffn_", ""): np.asarray(v) for k, v in inputs.items()}
    cc = np.ascontiguousarray
    vectors = [g[n] for n in ("time_decay", "time_first", "tmk", "tmv", "tmr", "ln1_w", "ln1_b", "ln2_w", "ln2_b",
                              "cmk", "cmr")]
    arrays = {
        "x_in": cc(g["x"].reshape(BATCHES * TOK, C)),
        "vectors": cc(np.stack(vectors, axis=1)),
        "ln0_w": cc(g["ln0_w"]), "ln0_b": cc(g["ln0_b"]),
        "w_att": cc(np.concatenate([g[n].T for n in ("Wk", "Wv", "Wr", "Wo", "Wfr")], axis=1)),
        "w_ffn_k": cc(g["Wfk"].T),
        "w_ffn_v": cc(g["Wfv"].T.reshape(HC, C, C).transpose(1, 0, 2).reshape(C, HC * C)),
        "w_exp": cc(g["We"].transpose(1, 0, 2).reshape(C, E * C)),
        "b_exp": cc(g["be"]),
        "w_gate": cc(g["Wg"]),
        "b_gate": cc(np.broadcast_to(g["bg"], (C, TILES, E)).reshape(C, TILES * E)),
        "ident": np.eye(C, dtype=np.float32),
    }
    nc = bacc.Bacc("TRN2", target_bir_lowering=False, num_devices=1)
    args = [nc.dram_tensor(f"in_{n}", v.shape, mybir.dt.from_np(v.dtype), kind="ExternalInput").ap()
            for n, v in arrays.items()]
    out = nc.dram_tensor("y_out", (BATCHES * TOK, C), F32, kind="ExternalOutput").ap()
    macaron_kernel(nc, *args, out)
    r = run_bass_kernel_spmd(nc, [{f"in_{n}": v for n, v in arrays.items()}], core_ids=[0])
    return r.results[0]["y_out"].reshape(BATCHES, TOK, C)
```

```python
from contextlib import ExitStack

import concourse.bass as bass
from concourse import mybir

ALU = mybir.AluOpType
ACT = mybir.ActivationFunctionType
AX_X = mybir.AxisListType.X
F32 = mybir.dt.float32

C = 128
BATCHES = 4
TOK = 512
TILES = TOK // C
E = 8
HALF = E // 2
HC = 4
EPS = 1e-5
WARM_UP = 5
LOWEST = -1e38
NEVER = -3.4e38

V_DECAY, V_FIRST, V_TMK, V_TMV, V_TMR, V_LN1W, V_LN1B, V_LN2W, V_LN2B, V_CMK, V_CMR = range(11)
NV = 11
MIXED = {"r": (2, V_TMR), "R": (4, V_CMR)}


def macaron_kernel(nc, x, vectors, ln0_w, ln0_b, w_att, w_ffn_k, w_ffn_v, w_exp, b_exp, w_gate, b_gate, ident_in, out):
    with ExitStack() as ctx:
        def sb(name, *shape):
            return ctx.enter_context(nc.sbuf_tensor(name, list(shape), F32))

        def sem(name):
            return ctx.enter_context(nc.semaphore(name))

        X = sb("X", C, BATCHES * TOK)
        X1 = sb("X1", C, BATCHES * TOK)
        X0 = sb("X0", C, BATCHES * TOK)
        X2 = sb("X2", C, BATCHES * TOK)
        Y = sb("Y", C, BATCHES * TOK)
        ident = sb("ident", C, C)
        vec = sb("vec", C, NV)
        w0b = sb("w0b", C, C)
        b0b = sb("b0b", C, C)
        watt = sb("watt", C, 5 * C)
        ones = sb("ones", C, NV)
        unmix = sb("unmix", C, NV)
        w_now = {n: sb(f"w_now_{n}", C, C)[:, :] for n in MIXED}
        w_before = {n: sb(f"w_before_{n}", C, C)[:, :] for n in MIXED}
        wfk = sb("wfk", C, HC * C)
        wfv = sb("wfv", C, HC * C)
        wexp = sb("wexp", C, E * C)
        bexp = sb("bexp", TILES * E, TILES * C)
        wgate = sb("wgate", C, E)
        bgate = sb("bgate", C, TILES * E)
        mhalf = sb("mhalf", C, TILES)
        decay = sb("decay", C, 1)
        warm = sb("warm", C, 1)
        decay_w = sb("decay_w", C, TOK)
        stats = sb("stats", C, TILES * 6)
        mv = sb("mv", C, TILES * 2)
        statsA = sb("statsA", C, TILES * 6)
        mvA = sb("mvA", C, TILES * 2)
        rstds = [sb(f"rstds{f}", C, BATCHES * TILES) for f in range(3)]
        shifts = [sb(f"shifts{f}", C, BATCHES * TILES) for f in range(3)]
        vtmp = sb("vtmp", C, TILES)
        vtmpA = sb("vtmpA", C, TILES)
        negmeanA = sb("negmeanA", C, TILES)
        xn = sb("xn", C, TOK)
        xnT = sb("xnT", C, TOK)
        xnG = sb("xnG", C, TOK)
        negmean = sb("negmean", C, TILES)
        logit = sb("logit", C, TILES * E)
        top = sb("top", C, TILES * E)
        top2 = sb("top2", C, TILES * E)
        rest = sb("rest", C, TILES * E)
        shifted = sb("shifted", C, TILES * E)
        expo = sb("expo", C, TILES * E)
        chosen = sb("chosen", C, TILES * E)
        gsum = sb("gsum", C, TILES)
        ginv = sb("ginv", C, TILES)
        gate_next = sb("gate_next", C, TILES * E)
        gate = sb("gate", C, TILES * E)
        gateT = sb("gateT", TILES * E, C)
        base = sb("base", C, TOK)
        acc = sb("acc", C, 2 * C)
        prod = sb("prod", C, 2 * HALF * C)
        pair = sb("pair", C, 2 * C)
        psum1 = sb("psum1", C, C)
        n2 = sb("n2", C, TOK)
        t0 = sb("t0", C, TOK)
        stats2 = sb("stats2", C, TILES * 6)
        mv2 = sb("mv2", C, TILES * 2)
        stats3 = sb("stats3", C, TILES * 6)
        mv3 = sb("mv3", C, TILES * 2)
        rstd2 = sb("rstd2", C, TILES)
        vtmp2 = sb("vtmp2", C, TILES)
        rstd3 = sb("rstd3", C, TILES)
        vtmp3 = sb("vtmp3", C, TILES)
        negmean2 = sb("negmean2", C, TILES)
        shift2 = sb("shift2", C, TILES)
        negmean3 = sb("negmean3", C, TILES)
        shift3 = sb("shift3", C, TILES)
        n1 = sb("n1", C, TOK)
        h1 = sb("h1", C, TOK + 1)
        dh = sb("dh", C, TOK)
        xk = sb("xk", C, TOK)
        xv = sb("xv", C, TOK)
        kS = sb("kS", C, TOK)
        vS = sb("vS", C, TOK)
        th = sb("th", C, TOK)
        PP = sb("PP", C, TOK + 1)
        q = sb("q", C, TOK)
        qq = sb("qq", C, 2 * TOK)
        de = sb("de", C, 2 * TOK)
        z = sb("z", C, TOK)
        zz = sb("zz", C, 2 * TOK)
        e12 = sb("e12", C, 3 * TOK)
        ev = sb("ev", C, TOK)
        AB = sb("AB", C, 2 * (TOK + 1))
        nd0 = sb("nd0", C, 2 * TOK)
        nd = sb("nd", C, 2 * TOK)
        rden = sb("rden", C, TOK)
        att = sb("att", C, TOK)
        sa = sb("sa", C, TOK)
        XR = sb("XR", C, TOK)
        xs = sb("xs", C, TOK)
        n3 = sb("n3", C, TOK)
        h2 = sb("h2", C, TOK + 1)
        dh2 = sb("dh2", C, TOK)
        xk2 = sb("xk2", C, TOK)
        rl = sb("rl", C, HC * TOK)
        kf = sb("kf", C, HC * TOK)
        th2 = sb("th2", C, TOK)
        rkv = sb("rkv", C, TOK)

        bank = [ctx.enter_context(nc.psum_tensor(f"bank{i}", [C, TOK], F32)) for i in range(8)]
        ps_exp = [bank[5], bank[3]], [bank[6], bank[4]]
        ps_xT, ps_gate, ps_base = bank[0], bank[1], bank[2]
        ps_k, ps_v, ps_r, ps_o = bank[0], bank[1], bank[2], bank[7]
        ps_hT, ps_h2T = bank[0], bank[7]
        ps_kf = [bank[5], bank[6]]
        ps_r2, ps_kv = bank[3], bank[4]

        s_x = [sem(f"x_loaded{b}") for b in range(BATCHES)]
        s_id = sem("ident_loaded")
        s_wg = sem("gate_weights_loaded")
        s_we = sem("expert_weights_loaded")
        s_be = sem("expert_biases_loaded")
        s_vec = sem("vectors_loaded")
        s_wa = sem("attention_weights_loaded")
        s_z = sem("bias_block_zeroed")
        s_const = sem("pool_constants_set")
        s_pres = sem("dve_constants_set")
        s_warm = sem("table_warmer_set")
        s_mixw = sem("mixed_weights_made")
        s_dec = sem("decay_exponential")
        s_out = sem("output_stored")

        s_passed_dve = sem("dve_wait_passed")
        s_passed_pool = sem("pool_wait_passed")

        MOE = ("stats meanvar var_eps rstd shift norm xT xG xT_copied logits gate_step shifted exp gateT gateT_copied bias "
               "gate base exp_lo exp_hi scaled pair psum1 out").split()
        ATT = ("stats meanvar var_eps rstd shift n2 x0_scaled X0 stats2 meanvar2 var2_eps rstd2 shift2 n1 hT h1 diff mixed_k mixed_v "
               "k v r k_copied v_copied th pp q z qq zz de e12 ev sumA sumB old e2v nd rden att sa o XR stats3 meanvar3 "
               "var3_eps rstd3 shift3 n3 h2T h2 diff2 mixed2_k kf relu kf2 r2 th2 kv xs rkv out").split()
        moe = [{n: sem(f"moe{f}_{n}") for n in MOE} for f in range(2)]
        for f in range(2):
            moe[f]["combine"] = [sem(f"moe{f}_combine{t}") for t in range(TILES)]
        a = {n: sem(f"att_{n}") for n in ATT}

        SRC, DST = (X, X2), (X1, Y)
        G = 9
        lo, hi = slice(0, TOK), slice(TOK, 2 * TOK)

        def seq(t, b, lo=0, n=TOK):
            return t[:, bass.ds(b * TOK + lo, n)]

        def grp(ap, n):
            return ap.rearrange("p (t n) -> p t n", n=n)

        def wait_if(eng, s, v):
            if not isinstance(v, int) or v > 0:
                eng.wait_ge(s, v)

        block = ctx.enter_context(nc.Block())

        @block.sync
        def _(sp):
            xin = x.rearrange("(b t p) c -> p b t c", t=TILES, p=C)
            dst = X[:, :].rearrange("p (b t c) -> p b t c", b=BATCHES, t=TILES)
            sp.dma_start(dst[:, 0], xin[:, 0]).then_inc(s_x[0], 16)
            sp.dma_start(ident[:, :], ident_in).then_inc(s_id, 16)
            sp.dma_start(wgate[:, :], w_gate).then_inc(s_wg, 16)
            sp.dma_start(bgate[:, :], b_gate).then_inc(s_wg, 16)
            sp.dma_start(dst[:, 1], xin[:, 1]).then_inc(s_x[1], 16)
            sp.wait_ge(s_z, 1)
            for t in range(TILES):
                sp.dma_start(bexp[t * E:(t + 1) * E, t * C:(t + 1) * C], b_exp).then_inc(s_be, 16)
            sp.dma_start(wexp[:, :], w_exp).then_inc(s_we, 16)
            for b in range(2, BATCHES):
                sp.dma_start(dst[:, b], xin[:, b]).then_inc(s_x[b], 16)
            sp.dma_start(vec[:, :], vectors).then_inc(s_vec, 16)
            sp.dma_start(w0b[:, :], ln0_w.partition_broadcast(C)).then_inc(s_vec, 16)
            sp.dma_start(b0b[:, :], ln0_b.partition_broadcast(C)).then_inc(s_vec, 16)
            sp.dma_start(watt[:, :], w_att).then_inc(s_wa, 16)
            sp.dma_start(wfk[:, :], w_ffn_k).then_inc(s_wa, 16)
            sp.dma_start(wfv[:, :], w_ffn_v).then_inc(s_wa, 16)
            yout = out.rearrange("(b t p) c -> p b t c", t=TILES, p=C)
            ysb = Y[:, :].rearrange("p (b t c) -> p b t c", b=BATCHES, t=TILES)
            for b in range(BATCHES):
                sp.wait_ge(moe[1]["out"], TILES * (b + 1))
                sp.dma_start(yout[:, b], ysb[:, b]).then_inc(s_out, 16)
            sp.wait_ge(s_out, 16 * BATCHES)

        @block.tensor
        def _(pe):
            def moe_transposes(f, b):
                m = moe[f]
                wait_if(pe, m["xT_copied"], TILES * b)
                pe.wait_ge(m["norm"], b + 1)
                for t in range(TILES):
                    mm = pe.transpose(ps_xT[:, t * C:(t + 1) * C], xn[:, t * C:(t + 1) * C], ident[:, :])
                mm.then_inc(m["xT"], 1)

            def moe_logits(f, b):
                m = moe[f]
                pe.wait_ge(m["xG"], b + 1)
                for t in range(TILES):
                    mm = pe.matmul(ps_gate[:, t * E:(t + 1) * E], xnG[:, t * C:(t + 1) * C], wgate[:, :],
                                   start=True, stop=True)
                mm.then_inc(m["logits"], 1)

            def moe_gateT(f, b):
                m = moe[f]
                pe.wait_ge(m["gate_step"], G * b + 9)
                pe.transpose(ps_gate[0:TILES * E, C:2 * C], gate_next[:, :], ident[:, :]).then_inc(m["gateT"], 1)

            def moe_bias(f, b):
                m = moe[f]
                pe.wait_ge(m["gateT_copied"], b + 1)
                pe.matmul(ps_base[:, :], gateT[:, :], bexp[:, :], start=True, stop=True).then_inc(m["bias"], 1)

            def moe_experts_lo(f, b, t):
                m = moe[f]
                pe.wait_ge(m["xT_copied"], TILES * b + t + 1)
                wait_if(pe, m["combine"][(t - 2) % TILES], HALF * (b + t // 2))
                pe.matmul(ps_exp[0][t % 2][:, :], xnT[:, t * C:(t + 1) * C], wexp[:, 0:HALF * C],
                          start=True, stop=True).then_inc(m["exp_lo"], 1)

            def moe_experts_hi(f, b, t):
                m = moe[f]
                wait_if(pe, m["scaled"], TILES * b + t - 1)
                pe.matmul(ps_exp[1][t % 2][:, :], xnT[:, t * C:(t + 1) * C], wexp[:, HALF * C:E * C],
                          start=True, stop=True).then_inc(m["exp_hi"], 1)

            def att_transpose(b):
                pe.wait_ge(a["n1"], b + 1)
                for t in range(TILES):
                    mm = pe.transpose(ps_hT[:, t * C:(t + 1) * C], n1[:, t * C:(t + 1) * C], ident[:, :])
                mm.then_inc(a["hT"], 1)

            def att_k(b):
                pe.wait_ge(a["mixed_k"], b + 1)
                pe.matmul(ps_k[:, :], watt[:, 0:C], xk[:, :], start=True, stop=True).then_inc(a["k"], 1)

            def att_v(b):
                pe.wait_ge(a["mixed_v"], b + 1)
                pe.matmul(ps_v[:, :], watt[:, C:2 * C], xv[:, :], start=True, stop=True).then_inc(a["v"], 1)

            def att_r(b):
                pe.wait_ge(a["h1"], b + 1)
                pe.matmul(ps_r[:, :], w_now["r"], h1[:, 1:TOK + 1], start=True, stop=False)
                pe.matmul(ps_r[:, :], w_before["r"], h1[:, 0:TOK], start=False, stop=True).then_inc(a["r"], 1)

            def att_o(b):
                pe.wait_ge(a["sa"], b + 1)
                for t in range(TILES):
                    mm = pe.matmul(ps_o[:, t * C:(t + 1) * C], sa[:, t * C:(t + 1) * C], watt[:, 3 * C:4 * C],
                                   start=True, stop=True)
                mm.then_inc(a["o"], 1)

            def att_transpose2(b):
                pe.wait_ge(a["n3"], b + 1)
                for t in range(TILES):
                    mm = pe.transpose(ps_h2T[:, t * C:(t + 1) * C], n3[:, t * C:(t + 1) * C], ident[:, :])
                mm.then_inc(a["h2T"], 1)

            def att_kf(b, j):
                if j == 0:
                    pe.wait_ge(a["mixed2_k"], b + 1)
                if j >= 2:
                    wait_if(pe, a["relu"], TILES * b + j - 1)
                pe.matmul(ps_kf[j % 2][:, :], wfk[:, j * C:(j + 1) * C], xk2[:, :],
                          start=True, stop=True).then_inc(a["kf"], 1)

            def att_r2(b):
                pe.wait_ge(a["h2"], b + 1)
                for t in range(TILES):
                    out_t = ps_r2[:, t * C:(t + 1) * C]
                    pe.matmul(out_t, h2[:, t * C + 1:(t + 1) * C + 1], w_now["R"], start=True, stop=False)
                    mm = pe.matmul(out_t, h2[:, t * C:(t + 1) * C], w_before["R"], start=False, stop=True)
                mm.then_inc(a["r2"], 1)

            def att_kv(b, j):
                pe.wait_ge(a["kf2"], TILES * b + j + 1)
                for t in range(TILES):
                    mm = pe.matmul(ps_kv[:, t * C:(t + 1) * C], kf[:, j * TOK + t * C:j * TOK + (t + 1) * C],
                                   wfv[:, j * C:(j + 1) * C], start=(j == 0 and t == 0), stop=(j == HC - 1 and t == TILES - 1))
                mm.then_inc(a["kv"], 1)

            pe.wait_ge(s_pres, 7)
            for _ in range(WARM_UP):
                pe.matmul(bank[4][:, :], decay_w[:, 0:C], decay_w[:, :], start=True, stop=True)
            pe.wait_ge(s_id, 16)
            moe_transposes(0, 0)
            pe.wait_ge(s_wg, 32)
            moe_logits(0, 0)
            pe.wait_ge(s_we, 16)
            moe_experts_lo(0, 0, 0)
            moe_experts_lo(0, 0, 1)
            moe_experts_hi(0, 0, 0)
            moe_transposes(0, 1)
            moe_gateT(0, 0)
            pe.wait_ge(s_be, 16 * TILES)
            moe_bias(0, 0)
            moe_experts_hi(0, 0, 1)
            moe_logits(0, 1)
            moe_experts_hi(0, 0, 2)
            moe_experts_hi(0, 0, 3)
            moe_experts_lo(0, 0, 2)
            moe_experts_lo(0, 0, 3)
            moe_gateT(0, 1)
            with pe.Fori(1, BATCHES - 1) as b:
                moe_experts_hi(0, b, 0)
                moe_bias(0, b)
                moe_experts_lo(0, b, 0)
                moe_transposes(0, b + 1)
                moe_experts_lo(0, b, 1)
                moe_experts_hi(0, b, 1)
                moe_logits(0, b + 1)
                moe_experts_hi(0, b, 2)
                moe_experts_lo(0, b, 2)
                moe_experts_hi(0, b, 3)
                moe_experts_lo(0, b, 3)
                moe_gateT(0, b + 1)
            moe_bias(0, 3)
            moe_experts_lo(0, 3, 0)
            for t in range(3):
                moe_experts_hi(0, 3, t)
            moe_experts_lo(0, 3, 1)
            moe_experts_lo(0, 3, 2)
            att_transpose(0)
            moe_experts_lo(0, 3, 3)
            moe_experts_hi(0, 3, 3)
            pe.wait_ge(s_wa, 48)
            att_k(0)
            att_v(0)
            pe.wait_ge(s_mixw, 5)
            att_r(0)
            att_transpose(1)
            att_r(1)
            att_k(1)
            att_v(1)
            with pe.Fori(1, BATCHES - 1) as b:
                att_o(b - 1)
                att_transpose2(b - 1)
                att_r2(b - 1)
                att_transpose(b + 1)
                for j in range(3):
                    att_kf(b - 1, j)
                att_kv(b - 1, 0)
                att_kv(b - 1, 1)
                att_kf(b - 1, 3)
                att_kv(b - 1, 2)
                att_v(b + 1)
                att_kv(b - 1, 3)
                att_k(b + 1)
                att_r(b + 1)
            att_o(2)
            moe_transposes(1, 0)
            moe_logits(1, 0)
            att_transpose2(2)
            att_r2(2)
            att_kf(2, 0)
            att_kf(2, 1)
            moe_gateT(1, 0)
            att_kf(2, 2)
            att_kf(2, 3)
            moe_bias(1, 0)
            pe.wait_ge(a["relu"], 11)
            moe_experts_lo(1, 0, 0)
            att_o(3)
            att_kv(2, 0)
            pe.wait_ge(a["relu"], 12)
            moe_experts_hi(1, 0, 0)
            att_kv(2, 1)
            moe_experts_lo(1, 0, 1)
            att_kv(2, 2)
            moe_transposes(1, 1)
            att_kv(2, 3)
            moe_experts_lo(1, 0, 2)
            att_transpose2(3)
            pe.wait_ge(a["rkv"], 3)
            moe_experts_hi(1, 0, 1)
            moe_experts_hi(1, 0, 2)
            moe_logits(1, 1)
            moe_experts_lo(1, 0, 3)
            att_kf(3, 0)
            pe.wait_ge(moe[1]["scaled"], 3)
            att_kf(3, 1)
            moe_experts_hi(1, 0, 3)
            att_kf(3, 2)
            att_kf(3, 3)
            pe.wait_ge(moe[1]["scaled"], 4)
            att_kv(3, 0)
            pe.wait_ge(moe[1]["combine"][3], 4)
            att_r2(3)
            att_kv(3, 1)
            moe_gateT(1, 1)
            att_kv(3, 2)
            att_kv(3, 3)
            pe.wait_ge(a["rkv"], 4)
            with pe.Fori(1, BATCHES - 1) as b:
                moe_experts_hi(1, b, 0)
                moe_bias(1, b)
                moe_experts_lo(1, b, 0)
                moe_transposes(1, b + 1)
                moe_experts_lo(1, b, 1)
                moe_experts_hi(1, b, 1)
                moe_logits(1, b + 1)
                moe_experts_hi(1, b, 2)
                moe_experts_lo(1, b, 2)
                moe_experts_hi(1, b, 3)
                moe_experts_lo(1, b, 3)
                moe_gateT(1, b + 1)
            moe_experts_hi(1, 3, 0)
            moe_bias(1, 3)
            moe_experts_lo(1, 3, 0)
            moe_experts_hi(1, 3, 1)
            moe_experts_lo(1, 3, 1)
            moe_experts_hi(1, 3, 2)
            moe_experts_hi(1, 3, 3)
            moe_experts_lo(1, 3, 2)
            moe_experts_lo(1, 3, 3)

        @block.vector
        def _(dve):
            def settled():
                dve.sem_inc(s_passed_dve, 1)

            def moe_stats(f, b):
                m = moe[f]
                if f == 0:
                    wait_if(dve, m["meanvar"], b)
                if f == 1:
                    dve.wait_ge(a["out"], b + 1)
                settled()
                for t in range(TILES):
                    i = dve.bn_stats(stats[:, t * 6:(t + 1) * 6], seq(SRC[f], b, t * C, C))
                i.then_inc(m["stats"], 1)

            def moe_meanvar(f, b):
                m = moe[f]
                dve.wait_ge(m["stats"], b + 1)
                if f == 0:
                    wait_if(dve, m["var_eps"], b)
                settled()
                for t in range(TILES):
                    i = dve.bn_aggr(mv[:, t * 2:(t + 1) * 2], stats[:, t * 6:(t + 1) * 6])
                i.then_inc(m["meanvar"], 1)

            def att_stats(b):
                dve.wait_ge(moe[0]["out"], TILES * b + 4)
                settled()
                for t in range(TILES):
                    i = dve.bn_stats(statsA[:, t * 6:(t + 1) * 6], seq(X1, b, t * C, C))
                i.then_inc(a["stats"], 1)

            def att_meanvar(b):
                dve.wait_ge(a["stats"], b + 1)
                settled()
                for t in range(TILES):
                    i = dve.bn_aggr(mvA[:, t * 2:(t + 1) * 2], statsA[:, t * 6:(t + 1) * 6])
                i.then_inc(a["meanvar"], 1)

            def att_stats2(b):
                dve.wait_ge(a["X0"], b + 1)
                settled()
                for t in range(TILES):
                    i = dve.bn_stats(stats2[:, t * 6:(t + 1) * 6], seq(X0, b, t * C, C))
                i.then_inc(a["stats2"], 1)

            def att_meanvar2(b):
                dve.wait_ge(a["stats2"], b + 1)
                settled()
                for t in range(TILES):
                    i = dve.bn_aggr(mv2[:, t * 2:(t + 1) * 2], stats2[:, t * 6:(t + 1) * 6])
                i.then_inc(a["meanvar2"], 1)

            def att_stats3(b):
                dve.wait_ge(a["XR"], b + 1)
                settled()
                for t in range(TILES):
                    i = dve.bn_stats(stats3[:, t * 6:(t + 1) * 6], XR[:, t * C:(t + 1) * C])
                i.then_inc(a["stats3"], 1)

            def att_meanvar3(b):
                dve.wait_ge(a["stats3"], b + 1)
                settled()
                for t in range(TILES):
                    i = dve.bn_aggr(mv3[:, t * 2:(t + 1) * 2], stats3[:, t * 6:(t + 1) * 6])
                i.then_inc(a["meanvar3"], 1)

            def moe_gates(f, b, k):
                m = moe[f]
                def step(i):
                    i.then_inc(m["gate_step"], 1)
                if k:
                    dve.wait_ge(m["gate_step"], G * b + k)
                if k == 0:
                    dve.wait_ge(m["logits"], b + 1)
                    step(dve.tensor_tensor(logit[:, :], ps_gate[:, 0:TILES * E], bgate[:, :], ALU.add))
                elif k == 1:
                    settled()
                    for t in range(TILES):
                        i = dve.max(top[:, t * E:(t + 1) * E], logit[:, t * E:(t + 1) * E])
                    step(i)
                elif k == 2:
                    dve.tensor_tensor(grp(shifted[:, :], E), grp(logit[:, :], E),
                                      grp(top[:, :], E)[:, :, 0:1].to_broadcast([C, TILES, E]),
                                      ALU.subtract).then_inc(m["shifted"], 1)
                    step(dve.tensor_copy(grp(top2[:, :], E)[:, :, 0:2], grp(top[:, :], E)[:, :, 0:2]))
                elif k == 3:
                    settled()
                    for t in range(TILES):
                        s = slice(t * E, (t + 1) * E)
                        i = dve.match_replace(rest[:, s], top2[:, s], logit[:, s], NEVER)
                    step(i)
                elif k == 4:
                    step(dve.tensor_tensor(chosen[:, :], logit[:, :], rest[:, :], ALU.not_equal))
                elif k == 5:
                    dve.wait_ge(m["exp"], b + 1)
                    step(dve.tensor_tensor(chosen[:, :], expo[:, :], chosen[:, :], ALU.mult))
                elif k == 6:
                    step(dve.tensor_reduce(gsum[:, :], grp(chosen[:, :], E), AX_X, ALU.add))
                elif k == 7:
                    step(dve.reciprocal(ginv[:, :], gsum[:, :]))
                else:
                    dve.wait_ge(m["gate_step"], G * b + 8)
                    step(dve.scalar_tensor_tensor(grp(gate_next[:, :], E), grp(chosen[:, :], E), 0.5,
                                                  ginv[:, :].unsqueeze(2).to_broadcast([C, TILES, E]),
                                                  ALU.mult, ALU.mult))

            def moe_take_gates(f, b):
                m = moe[f]
                dve.wait_ge(m["gate_step"], G * b + 9)
                wait_if(dve, m["scaled"], TILES * b)
                wait_if(dve, m["combine"][3], HALF * b)
                dve.tensor_copy(gate[:, :], gate_next[:, :]).then_inc(m["gate"], 1)

            def moe_base(f, b):
                m = moe[f]
                dve.wait_ge(m["bias"], b + 1)
                dve.tensor_tensor(base[:, :], ps_base[:, :], seq(SRC[f], b), ALU.add).then_inc(m["base"], 1)

            def moe_combine(f, b, t, e):
                m = moe[f]
                half = acc[:, (t % 2) * C:(t % 2 + 1) * C]
                if e == 0:
                    wait_if(dve, m["out"], TILES * b + t - 1)
                    if t == 0:
                        dve.wait_ge(m["gate"], b + 1)
                    dve.wait_ge(m["exp_lo"], TILES * b + t + 1)
                    if t == 0:
                        dve.wait_ge(m["base"], b + 1)
                else:
                    dve.wait_ge(m["combine"][t], HALF * b + e)
                dve.scalar_tensor_tensor(half, ps_exp[0][t % 2][:, e * C:(e + 1) * C], gate[:, t * E + e:t * E + e + 1],
                                         base[:, t * C:(t + 1) * C] if e == 0 else half,
                                         ALU.mult, ALU.add).then_inc(m["combine"][t], 1)

            def att_diff(b):
                dve.wait_ge(a["h1"], b + 1)
                dve.tensor_tensor(dh[:, :], h1[:, 1:TOK + 1], h1[:, 0:TOK], ALU.subtract).then_inc(a["diff"], 1)

            def att_mix_k(b):
                dve.wait_ge(a["diff"], b + 1)
                dve.scalar_tensor_tensor(xk[:, :], dh[:, :], vec[:, V_TMK:V_TMK + 1], h1[:, 0:TOK],
                                         ALU.mult, ALU.add).then_inc(a["mixed_k"], 1)

            def att_mix_v(b):
                dve.scalar_tensor_tensor(xv[:, :], dh[:, :], vec[:, V_TMV:V_TMV + 1], h1[:, 0:TOK],
                                         ALU.mult, ALU.add).then_inc(a["mixed_v"], 1)

            def att_maximum(b):
                dve.wait_ge(a["k_copied"], b + 1)
                dve.tensor_tensor_scan(PP[:, 1:TOK + 1], decay_w[:, :], kS[:, :], LOWEST, ALU.add, ALU.max).then_inc(a["pp"], 1)

            def att_q(b):
                dve.wait_ge(a["pp"], b + 1)
                dve.scalar_tensor_tensor(q[:, :], PP[:, 0:TOK], decay[:, 0:1], kS[:, :], ALU.add, ALU.subtract).then_inc(a["q"], 1)

            def att_z(b):
                dve.scalar_tensor_tensor(z[:, :], kS[:, :], vec[:, V_FIRST:V_FIRST + 1], PP[:, 0:TOK],
                                         ALU.add, ALU.subtract).then_inc(a["z"], 1)

            def att_ev(b):
                dve.wait_ge(a["de"], b + 1)
                dve.tensor_tensor(ev[:, :], de[:, hi], vS[:, :], ALU.mult).then_inc(a["ev"], 1)

            def att_sum_ones(b):
                dve.tensor_tensor_scan(AB[:, TOK + 2:2 * TOK + 2], de[:, lo], de[:, hi], 0.0, ALU.mult, ALU.add).then_inc(a["sumB"], 1)

            def att_sum_v(b):
                dve.wait_ge(a["ev"], b + 1)
                dve.tensor_tensor_scan(AB[:, 1:TOK + 1], de[:, lo], ev[:, :], 0.0, ALU.mult, ALU.add).then_inc(a["sumA"], 1)

            def att_old(b):
                dve.wait_ge(a["sumA"], b + 1)
                dve.wait_ge(a["e12"], b + 1)
                dve.wait_ge(a["sumB"], b + 1)
                ab = AB[:, :].rearrange("p (s n) -> p s n", s=2)[:, :, 0:TOK]
                dve.tensor_tensor(grp(nd0[:, :], TOK), ab, e12[:, lo].unsqueeze(1).to_broadcast([C, 2, TOK]),
                                  ALU.mult).then_inc(a["old"], 1)

            def att_new(b):
                dve.wait_ge(a["e2v"], b + 1)
                dve.wait_ge(a["old"], b + 1)
                dve.tensor_tensor(nd[:, :], nd0[:, :], e12[:, TOK:3 * TOK], ALU.add).then_inc(a["nd"], 1)

            def att_reciprocal(b):
                dve.wait_ge(a["nd"], b + 1)
                dve.reciprocal(rden[:, :], nd[:, hi]).then_inc(a["rden"], 1)

            def att_att(b):
                dve.wait_ge(a["rden"], b + 1)
                dve.tensor_tensor(att[:, :], nd[:, lo], rden[:, :], ALU.mult).then_inc(a["att"], 1)

            def att_sa(b):
                dve.wait_ge(a["th"], b + 1)
                dve.wait_ge(a["att"], b + 1)
                dve.scalar_tensor_tensor(sa[:, :], th[:, :], 1.0, att[:, :], ALU.add, ALU.mult).then_inc(a["sa"], 1)

            def att_resid(b):
                dve.wait_ge(a["o"], b + 1)
                dve.scalar_tensor_tensor(XR[:, :], ps_o[:, :], 0.5, seq(X0, b), ALU.mult, ALU.add).then_inc(a["XR"], 1)

            def att_diff2(b):
                dve.wait_ge(a["h2"], b + 1)
                dve.tensor_tensor(dh2[:, :], h2[:, 1:TOK + 1], h2[:, 0:TOK], ALU.subtract).then_inc(a["diff2"], 1)

            def att_mix2_k(b):
                dve.wait_ge(a["diff2"], b + 1)
                dve.scalar_tensor_tensor(xk2[:, :], dh2[:, :], vec[:, V_CMK:V_CMK + 1], h2[:, 0:TOK],
                                         ALU.mult, ALU.add).then_inc(a["mixed2_k"], 1)

            def att_rkv(b):
                dve.wait_ge(a["th2"], b + 1)
                dve.wait_ge(a["kv"], TILES * b + 4)
                dve.scalar_tensor_tensor(rkv[:, :], th2[:, :], 1.0, ps_kv[:, :], ALU.add, ALU.mult).then_inc(a["rkv"], 1)

            def att_out(b):
                dve.wait_ge(a["xs"], b + 1)
                dve.wait_ge(a["rkv"], b + 1)
                dve.scalar_tensor_tensor(seq(X2, b), rkv[:, :], 0.5, xs[:, :], ALU.mult, ALU.add).then_inc(a["out"], 1)

            dve.memset(warm[:, :], 0.0).then_inc(s_warm, 1)
            for t, v in ((top2[:, :], NEVER), (h1[:, 0:1], 0.0), (h2[:, 0:1], 0.0), (PP[:, 0:1], LOWEST),
                         (AB[:, 0:1], 0.0), (AB[:, TOK + 1:TOK + 2], 0.0)):
                dve.memset(t, v).then_inc(s_pres, 1)
            dve.memset(decay_w[:, :], 0.0).then_inc(s_pres, 1)
            dve.wait_ge(s_pres, 7)
            dve.wait_ge(s_x[0], 16)
            moe_stats(0, 0)
            moe_meanvar(0, 0)
            dve.wait_ge(s_x[1], 16)
            moe_stats(0, 1)
            moe_meanvar(0, 1)
            dve.wait_ge(s_x[2], 16)
            moe_stats(0, 2)
            dve.wait_ge(s_wg, 32)
            for k in range(G):
                moe_gates(0, 0, k)
            moe_meanvar(0, 2)
            moe_take_gates(0, 0)
            dve.wait_ge(s_x[3], 16)
            moe_stats(0, 3)
            moe_meanvar(0, 3)
            moe_base(0, 0)
            moe_combine(0, 0, 0, 0)
            moe_combine(0, 0, 1, 0)
            moe_combine(0, 0, 0, 1)
            moe_combine(0, 0, 1, 1)
            moe_combine(0, 0, 0, 2)
            moe_gates(0, 1, 0)
            moe_combine(0, 0, 1, 2)
            moe_combine(0, 0, 0, 3)
            moe_gates(0, 1, 1)
            moe_combine(0, 0, 1, 3)
            for k in range(2, 9):
                moe_gates(0, 1, k)
            moe_combine(0, 0, 2, 0)
            moe_combine(0, 0, 2, 1)
            moe_combine(0, 0, 3, 0)
            moe_combine(0, 0, 2, 2)
            moe_combine(0, 0, 3, 1)
            moe_combine(0, 0, 2, 3)
            moe_combine(0, 0, 3, 2)
            moe_combine(0, 0, 3, 3)
            with dve.Fori(1, BATCHES - 1) as b:
                moe_take_gates(0, b)
                moe_base(0, b)
                moe_combine(0, b, 0, 0)
                att_stats(b - 1)
                att_meanvar(b - 1)
                moe_combine(0, b, 0, 1)
                moe_combine(0, b, 1, 0)
                moe_combine(0, b, 0, 2)
                moe_combine(0, b, 1, 1)
                moe_combine(0, b, 0, 3)
                moe_gates(0, b + 1, 0)
                moe_combine(0, b, 1, 2)
                for k in range(1, 5):
                    moe_gates(0, b + 1, k)
                moe_combine(0, b, 1, 3)
                moe_combine(0, b, 2, 0)
                for k in range(5, 9):
                    moe_gates(0, b + 1, k)
                moe_combine(0, b, 2, 1)
                moe_combine(0, b, 2, 2)
                moe_combine(0, b, 3, 0)
                moe_combine(0, b, 2, 3)
                for e in range(1, 4):
                    moe_combine(0, b, 3, e)
            moe_base(0, 3)
            moe_take_gates(0, 3)
            att_stats(2)
            dve.wait_ge(s_vec, 48)
            dve.wait_ge(s_dec, 1)
            dve.tensor_scalar(decay[:, :], decay[:, :], -1.0, None, ALU.mult).then_inc(s_dec, 1)
            dve.wait_ge(s_dec, 2)
            dve.tensor_scalar(decay_w[:, :], decay_w[:, :], decay[:, 0:1], None, ALU.add).then_inc(s_dec, 1)
            dve.wait_ge(s_dec, 3)
            moe_combine(0, 3, 0, 0)
            att_stats2(0)
            att_meanvar2(0)
            moe_combine(0, 3, 0, 1)
            moe_combine(0, 3, 1, 0)
            moe_combine(0, 3, 1, 1)
            moe_combine(0, 3, 0, 2)
            att_meanvar(2)
            moe_combine(0, 3, 1, 2)
            moe_combine(0, 3, 0, 3)
            moe_combine(0, 3, 2, 0)
            moe_combine(0, 3, 2, 1)
            moe_combine(0, 3, 1, 3)
            att_diff(0)
            att_mix_k(0)
            att_mix_v(0)
            att_stats2(1)
            moe_combine(0, 3, 3, 0)
            moe_combine(0, 3, 3, 1)
            att_maximum(0)
            att_q(0)
            att_meanvar2(1)
            moe_combine(0, 3, 2, 2)
            moe_combine(0, 3, 3, 2)
            att_z(0)
            moe_combine(0, 3, 2, 3)
            moe_combine(0, 3, 3, 3)
            att_ev(0)
            att_sum_ones(0)
            att_sum_v(0)
            att_old(0)
            att_new(0)
            att_reciprocal(0)
            att_diff(1)
            att_mix_k(1)
            att_mix_v(1)
            att_att(0)
            att_sa(0)
            att_stats(3)
            att_meanvar(3)
            with dve.Fori(1, BATCHES - 1) as b:
                att_maximum(b)
                att_resid(b - 1)
                att_stats3(b - 1)
                att_meanvar3(b - 1)
                att_q(b)
                att_z(b)
                att_stats2(b + 1)
                att_meanvar2(b + 1)
                att_diff2(b - 1)
                att_ev(b)
                att_mix2_k(b - 1)
                att_sum_v(b)
                att_sum_ones(b)
                att_old(b)
                att_new(b)
                att_diff(b + 1)
                att_mix_k(b + 1)
                att_mix_v(b + 1)
                att_reciprocal(b)
                att_att(b)
                att_sa(b)
                att_rkv(b - 1)
                att_out(b - 1)
                moe_stats(1, b - 1)
                moe_meanvar(1, b - 1)
            att_maximum(3)
            att_resid(2)
            att_stats3(2)
            att_meanvar3(2)
            att_q(3)
            for k in range(3):
                moe_gates(1, 0, k)
            att_z(3)
            moe_gates(1, 0, 3)
            moe_gates(1, 0, 4)
            att_ev(3)
            moe_gates(1, 0, 5)
            att_sum_v(3)
            moe_gates(1, 0, 6)
            att_diff2(2)
            att_sum_ones(3)
            moe_gates(1, 0, 7)
            att_mix2_k(2)
            att_old(3)
            moe_gates(1, 0, 8)
            att_new(3)
            att_reciprocal(3)
            att_att(3)
            moe_take_gates(1, 0)
            att_sa(3)
            moe_base(1, 0)
            moe_combine(1, 0, 0, 0)
            moe_combine(1, 0, 0, 1)
            att_resid(3)
            att_stats3(3)
            att_meanvar3(3)
            moe_combine(1, 0, 1, 0)
            moe_combine(1, 0, 0, 2)
            moe_combine(1, 0, 0, 3)
            att_rkv(2)
            moe_combine(1, 0, 1, 1)
            moe_combine(1, 0, 1, 2)
            moe_combine(1, 0, 2, 0)
            moe_combine(1, 0, 2, 1)
            moe_combine(1, 0, 1, 3)
            moe_combine(1, 0, 2, 2)
            att_diff2(3)
            moe_combine(1, 0, 2, 3)
            att_mix2_k(3)
            for k in range(3):
                moe_gates(1, 1, k)
            att_out(2)
            moe_gates(1, 1, 3)
            moe_stats(1, 2)
            moe_combine(1, 0, 3, 0)
            moe_gates(1, 1, 4)
            moe_combine(1, 0, 3, 1)
            moe_gates(1, 1, 5)
            moe_gates(1, 1, 6)
            moe_combine(1, 0, 3, 2)
            moe_gates(1, 1, 7)
            moe_meanvar(1, 2)
            moe_gates(1, 1, 8)
            moe_combine(1, 0, 3, 3)
            att_rkv(3)
            att_out(3)
            moe_stats(1, 3)
            moe_meanvar(1, 3)
            with dve.Fori(1, BATCHES - 1) as b:
                moe_base(1, b)
                moe_take_gates(1, b)
                moe_combine(1, b, 0, 0)
                moe_combine(1, b, 0, 1)
                moe_combine(1, b, 1, 0)
                moe_combine(1, b, 0, 2)
                moe_combine(1, b, 1, 1)
                moe_combine(1, b, 0, 3)
                moe_combine(1, b, 1, 2)
                for k in range(TILES):
                    moe_gates(1, b + 1, k)
                moe_combine(1, b, 1, 3)
                moe_gates(1, b + 1, 4)
                moe_gates(1, b + 1, 5)
                moe_combine(1, b, 2, 0)
                for k in range(6, 9):
                    moe_gates(1, b + 1, k)
                moe_combine(1, b, 2, 1)
                moe_combine(1, b, 2, 2)
                moe_combine(1, b, 3, 0)
                moe_combine(1, b, 2, 3)
                for e in range(1, 4):
                    moe_combine(1, b, 3, e)
            moe_take_gates(1, 3)
            moe_base(1, 3)
            for e in range(HALF):
                moe_combine(1, 3, 0, e)
            for e in range(HALF):
                moe_combine(1, 3, 1, e)
            for e in range(3):
                moe_combine(1, 3, 2, e)
            moe_combine(1, 3, 3, 0)
            moe_combine(1, 3, 2, 3)
            for e in range(1, 4):
                moe_combine(1, 3, 3, e)

        @block.scalar
        def _(act):
            def normalise(dst, src, rs, sh, s_done):
                for t in range(TILES):
                    i = act.activation(dst[:, t * C:(t + 1) * C], src(t), ACT.Identity, bias=sh(t), scale=rs(t))
                i.then_inc(s_done, 1)

            def one(t, b):
                return lambda i: t[:, bass.ds(b * TILES + i, 1)]

            def tile(t):
                return lambda i: t[:, i:i + 1]

            def moe_norm(f, b):
                m = moe[f]
                act.wait_ge(m["shift"], b + 1)
                normalise(xn, lambda t: seq(SRC[f], b, t * C, C), one(rstds[f], b), one(shifts[f], b), m["norm"])

            def moe_copy_xG(f, b):
                m = moe[f]
                act.wait_ge(m["xT"], b + 1)
                act.copy(xnG[:, :], ps_xT[:, :]).then_inc(m["xG"], 1)

            def moe_copy_xT(f, b, t):
                m = moe[f]
                if t < 4:
                    wait_if(act, m["exp_hi"], TILES * b + t - 3)
                if t < 4:
                    wait_if(act, m["exp_lo"], TILES * b + t - 3)
                if t == 0:
                    act.wait_ge(m["xT"], b + 1)
                act.copy(xnT[:, t * C:(t + 1) * C], ps_xT[:, t * C:(t + 1) * C]).then_inc(m["xT_copied"], 1)

            def moe_exp(f, b):
                m = moe[f]
                act.wait_ge(m["gate_step"], G * b + 3)
                act.activation(expo[:, :], shifted[:, :], ACT.Exp).then_inc(m["exp"], 1)

            def moe_copy_gateT(f, b):
                m = moe[f]
                act.wait_ge(m["gateT"], b + 1)
                act.copy(gateT[:, :], ps_gate[0:TILES * E, C:2 * C]).then_inc(m["gateT_copied"], 1)

            def moe_scale(f, b, t):
                m = moe[f]
                wait_if(act, m["pair"], TILES * b + t - 1)
                act.wait_ge(m["exp_hi"], TILES * b + t + 1)
                if t == 0:
                    act.wait_ge(m["gate"], b + 1)
                for e in range(HALF):
                    o = ((t % 2) * HALF + e) * C
                    i = act.activation(prod[:, o:o + C], ps_exp[1][t % 2][:, e * C:(e + 1) * C], ACT.Copy,
                                       scale=gate[:, t * E + HALF + e:t * E + HALF + e + 1])
                i.then_inc(m["scaled"], 1)

            def att_n2(b):
                wait_if(act, a["x0_scaled"], b)
                act.wait_ge(a["shift"], b + 2)
                normalise(n2, lambda t: seq(X1, b, t * C, C), one(rstds[2], b), one(shifts[2], b), a["n2"])

            def att_n1(b):
                act.wait_ge(a["shift2"], b + 1)
                normalise(n1, lambda t: seq(X0, b, t * C, C), tile(rstd2), tile(shift2), a["n1"])

            def att_n3(b):
                act.wait_ge(a["shift3"], b + 1)
                normalise(n3, lambda t: XR[:, t * C:(t + 1) * C], tile(rstd3), tile(shift3), a["n3"])

            def att_h1(b):
                act.wait_ge(a["hT"], b + 1)
                act.activation(h1[:, 1:TOK + 1], ps_hT[:, :], ACT.Identity, bias=vec[:, V_LN1B:V_LN1B + 1],
                               scale=vec[:, V_LN1W:V_LN1W + 1]).then_inc(a["h1"], 1)

            def att_h2(b):
                act.wait_ge(a["h2T"], b + 1)
                act.activation(h2[:, 1:TOK + 1], ps_h2T[:, :], ACT.Identity, bias=vec[:, V_LN2B:V_LN2B + 1],
                               scale=vec[:, V_LN2W:V_LN2W + 1]).then_inc(a["h2"], 1)

            def att_copy_k(b):
                act.wait_ge(a["k"], b + 1)
                act.copy(kS[:, :], ps_k[:, :]).then_inc(a["k_copied"], 1)

            def att_copy_v(b):
                act.wait_ge(a["v"], b + 1)
                act.copy(vS[:, :], ps_v[:, :]).then_inc(a["v_copied"], 1)

            def att_tanh(b):
                act.wait_ge(a["r"], b + 1)
                wait_if(act, a["sa"], b)
                act.activation(th[:, :], ps_r[:, :], ACT.Tanh, scale=0.5).then_inc(a["th"], 1)

            def att_relu_q(b):
                act.wait_ge(a["q"], b + 1)
                act.activation(qq[:, hi], q[:, :], ACT.Relu)
                act.activation(qq[:, lo], q[:, :], ACT.Relu, scale=-1.0).then_inc(a["qq"], 1)

            def att_relu_z(b):
                act.wait_ge(a["z"], b + 1)
                act.activation(zz[:, lo], z[:, :], ACT.Relu)
                act.activation(zz[:, hi], z[:, :], ACT.Relu, scale=-1.0).then_inc(a["zz"], 1)

            def att_exp_q(b):
                act.wait_ge(a["qq"], b + 1)
                act.activation(de[:, :], qq[:, :], ACT.Exp, scale=-1.0).then_inc(a["de"], 1)

            def att_exp_z(b):
                act.wait_ge(a["zz"], b + 1)
                act.activation(e12[:, :].rearrange("p (s n) -> p s n", s=3)[:, 0:3:2, :], grp(zz[:, :], TOK),
                               ACT.Exp, scale=-1.0).then_inc(a["e12"], 1)

            def att_relu(b, j):
                act.wait_ge(a["kf"], TILES * b + j + 1)
                act.activation(rl[:, j * TOK:(j + 1) * TOK], ps_kf[j % 2][:, :], ACT.Relu).then_inc(a["relu"], 1)

            def att_square(b, j):
                act.wait_ge(a["relu"], TILES * b + j + 1)
                act.activation(kf[:, j * TOK:(j + 1) * TOK], rl[:, j * TOK:(j + 1) * TOK], ACT.Square).then_inc(a["kf2"], 1)

            def att_tanh2(b):
                act.wait_ge(a["r2"], b + 1)
                act.activation(th2[:, :], ps_r2[:, :], ACT.Tanh, scale=0.5).then_inc(a["th2"], 1)

            act.wait_ge(s_warm, 1)
            act.activation(expo[:, 0:1], warm[:, :], ACT.Exp)
            act.wait_ge(s_pres, 7)
            moe_norm(0, 0)
            moe_copy_xG(0, 0)
            moe_copy_xT(0, 0, 0)
            moe_copy_xT(0, 0, 1)
            moe_norm(0, 1)
            moe_copy_xT(0, 0, 2)
            moe_exp(0, 0)
            moe_copy_xT(0, 0, 3)
            moe_copy_gateT(0, 0)
            moe_copy_xT(0, 1, 0)
            moe_scale(0, 0, 0)
            moe_copy_xG(0, 1)
            moe_copy_xT(0, 1, 1)
            moe_scale(0, 0, 1)
            moe_scale(0, 0, 2)
            moe_exp(0, 1)
            moe_copy_xT(0, 1, 2)
            act.wait_ge(s_vec, 48)
            act.activation(decay[:, :], vec[:, V_DECAY:V_DECAY + 1], ACT.Exp).then_inc(s_dec, 1)
            moe_scale(0, 0, 3)
            moe_copy_gateT(0, 1)
            moe_copy_xT(0, 1, 3)
            with act.Fori(1, BATCHES - 1) as b:
                moe_norm(0, b + 1)
                moe_scale(0, b, 0)
                moe_copy_xT(0, b + 1, 0)
                moe_copy_xG(0, b + 1)
                moe_scale(0, b, 1)
                moe_copy_xT(0, b + 1, 1)
                moe_scale(0, b, 2)
                moe_exp(0, b + 1)
                moe_copy_xT(0, b + 1, 2)
                moe_scale(0, b, 3)
                moe_copy_gateT(0, b + 1)
                moe_copy_xT(0, b + 1, 3)
            att_n2(0)
            moe_scale(0, 3, 0)
            moe_scale(0, 3, 1)
            att_n2(1)
            moe_scale(0, 3, 2)
            att_n1(0)
            att_h1(0)
            att_copy_k(0)
            moe_scale(0, 3, 3)
            att_copy_v(0)
            att_relu_q(0)
            att_exp_q(0)
            att_relu_z(0)
            att_exp_z(0)
            att_n1(1)
            att_tanh(0)
            att_h1(1)
            att_copy_k(1)
            att_copy_v(1)
            with act.Fori(1, BATCHES - 1) as b:
                att_tanh(b)
                att_n2(b + 1)
                att_relu_q(b)
                att_n3(b - 1)
                att_relu_z(b)
                att_h2(b - 1)
                att_exp_q(b)
                att_exp_z(b)
                att_n1(b + 1)
                att_h1(b + 1)
                att_relu(b - 1, 0)
                att_square(b - 1, 0)
                att_relu(b - 1, 1)
                att_square(b - 1, 1)
                att_tanh2(b - 1)
                att_relu(b - 1, 2)
                att_square(b - 1, 2)
                att_relu(b - 1, 3)
                att_square(b - 1, 3)
                att_copy_v(b + 1)
                att_copy_k(b + 1)
            moe_norm(1, 0)
            moe_copy_xG(1, 0)
            att_relu_q(3)
            att_n3(2)
            att_exp_q(3)
            moe_exp(1, 0)
            moe_copy_xT(1, 0, 0)
            att_h2(2)
            att_relu_z(3)
            att_exp_z(3)
            att_tanh(3)
            att_tanh2(2)
            moe_copy_xT(1, 0, 1)
            moe_copy_xT(1, 0, 2)
            att_relu(2, 0)
            att_relu(2, 1)
            att_square(2, 0)
            moe_copy_gateT(1, 0)
            att_square(2, 1)
            att_relu(2, 2)
            moe_norm(1, 1)
            att_square(2, 2)
            att_relu(2, 3)
            moe_copy_xT(1, 0, 3)
            moe_scale(1, 0, 0)
            att_square(2, 3)
            att_n3(3)
            moe_copy_xT(1, 1, 0)
            moe_copy_xG(1, 1)
            att_h2(3)
            moe_scale(1, 0, 1)
            moe_scale(1, 0, 2)
            moe_copy_xT(1, 1, 1)
            moe_copy_xT(1, 1, 2)
            att_relu(3, 0)
            att_square(3, 0)
            att_relu(3, 1)
            moe_exp(1, 1)
            moe_scale(1, 0, 3)
            att_relu(3, 2)
            att_relu(3, 3)
            for j in range(1, 4):
                att_square(3, j)
            att_tanh2(3)
            moe_copy_xT(1, 1, 3)
            moe_copy_gateT(1, 1)
            with act.Fori(1, BATCHES - 1) as b:
                moe_norm(1, b + 1)
                moe_copy_xG(1, b + 1)
                moe_copy_xT(1, b + 1, 0)
                moe_scale(1, b, 0)
                moe_copy_xT(1, b + 1, 1)
                moe_scale(1, b, 1)
                moe_exp(1, b + 1)
                moe_scale(1, b, 2)
                moe_copy_xT(1, b + 1, 2)
                moe_scale(1, b, 3)
                moe_copy_gateT(1, b + 1)
                moe_copy_xT(1, b + 1, 3)
            for t in range(TILES):
                moe_scale(1, 3, t)

        @block.gpsimd
        def _(pool):
            def four(t, b):
                return t[:, bass.ds(b * TILES, TILES)]

            def mix_weights():
                pool.tensor_tensor(unmix[:, :], ones[:, :], vec[:, :], ALU.subtract).then_inc(s_mixw, 1)
                pool.wait_ge(s_mixw, 1)
                for n, (i, v) in MIXED.items():
                    for dst, mix in ((w_now[n], vec), (w_before[n], unmix)):
                        pool.tensor_tensor(dst, watt[:, i * C:(i + 1) * C], mix[:, v:v + 1].to_broadcast([C, C]),
                                           ALU.mult).then_inc(s_mixw, 1)

            def moe_var(f, b):
                m = moe[f]
                pool.wait_ge(m["meanvar"], b + 1)
                if f == 0:
                    wait_if(pool, m["shift"], b)
                pool.sem_inc(s_passed_pool, 1)
                pool.tensor_scalar(vtmp[:, :], grp(mv[:, :], 2)[:, :, 1], 1.0, EPS, ALU.mult, ALU.add)
                pool.tensor_scalar(negmean[:, :], grp(mv[:, :], 2)[:, :, 0], -1.0, None, ALU.mult).then_inc(m["var_eps"], 1)

            def moe_rstd(f, b):
                m = moe[f]
                pool.wait_ge(m["var_eps"], b + 1)
                pool.tensor_tensor(four(rstds[f], b), vtmp[:, :], mhalf[:, :], ALU.pow).then_inc(m["rstd"], 1)

            def moe_shift(f, b):
                m = moe[f]
                pool.wait_ge(m["rstd"], b + 1)
                pool.tensor_tensor(four(shifts[f], b), negmean[:, :], four(rstds[f], b), ALU.mult).then_inc(m["shift"], 1)

            def att_var(b):
                wait_if(pool, a["shift"], b + 1)
                pool.wait_ge(a["meanvar"], b + 1)
                pool.sem_inc(s_passed_pool, 1)
                pool.tensor_scalar(vtmpA[:, :], grp(mvA[:, :], 2)[:, :, 1], 1.0 + EPS, EPS * EPS, ALU.mult, ALU.add)
                pool.tensor_scalar(negmeanA[:, :], grp(mvA[:, :], 2)[:, :, 0], -1.0, None, ALU.mult).then_inc(a["var_eps"], 1)

            def att_rstd(b):
                pool.wait_ge(a["var_eps"], b + 1)
                pool.tensor_tensor(four(rstds[2], b), vtmpA[:, :], mhalf[:, :], ALU.pow).then_inc(a["rstd"], 1)

            def att_shift(b):
                pool.wait_ge(a["rstd"], b + 1)
                pool.tensor_tensor(four(shifts[2], b), negmeanA[:, :], four(rstds[2], b), ALU.mult).then_inc(a["shift"], 1)

            def att_var2(b):
                pool.wait_ge(a["meanvar2"], b + 1)
                pool.sem_inc(s_passed_pool, 1)
                pool.tensor_scalar(vtmp2[:, :], grp(mv2[:, :], 2)[:, :, 1], 1.0, EPS, ALU.mult, ALU.add)
                pool.tensor_scalar(negmean2[:, :], grp(mv2[:, :], 2)[:, :, 0], -1.0, None, ALU.mult).then_inc(a["var2_eps"], 1)

            def att_rstd2(b):
                pool.wait_ge(a["var2_eps"], b + 1)
                pool.tensor_tensor(rstd2[:, :], vtmp2[:, :], mhalf[:, :], ALU.pow).then_inc(a["rstd2"], 1)

            def att_shift2(b):
                pool.wait_ge(a["rstd2"], b + 1)
                pool.tensor_tensor(shift2[:, :], negmean2[:, :], rstd2[:, :], ALU.mult).then_inc(a["shift2"], 1)

            def att_var3(b):
                pool.wait_ge(a["meanvar3"], b + 1)
                pool.sem_inc(s_passed_pool, 1)
                pool.tensor_scalar(vtmp3[:, :], grp(mv3[:, :], 2)[:, :, 1], 1.0, EPS, ALU.mult, ALU.add)
                pool.tensor_scalar(negmean3[:, :], grp(mv3[:, :], 2)[:, :, 0], -1.0, None, ALU.mult).then_inc(a["var3_eps"], 1)

            def att_rstd3(b):
                pool.wait_ge(a["var3_eps"], b + 1)
                pool.tensor_tensor(rstd3[:, :], vtmp3[:, :], mhalf[:, :], ALU.pow).then_inc(a["rstd3"], 1)

            def att_shift3(b):
                pool.wait_ge(a["rstd3"], b + 1)
                pool.tensor_tensor(shift3[:, :], negmean3[:, :], rstd3[:, :], ALU.mult).then_inc(a["shift3"], 1)

            def moe_pair(f, b, t):
                m = moe[f]
                pool.wait_ge(m["scaled"], TILES * b + t + 1)
                if t >= 1:
                    wait_if(pool, m["psum1"], TILES * b + t)
                o = (t % 2) * HALF * C
                pool.tensor_tensor(pair[:, :], prod[:, o:o + 2 * C], prod[:, o + 2 * C:o + 4 * C],
                                   ALU.add).then_inc(m["pair"], 1)

            def moe_psum1(f, b, t):
                m = moe[f]
                if t >= 1:
                    wait_if(pool, m["out"], TILES * b + t)
                pool.wait_ge(m["pair"], TILES * b + t + 1)
                pool.tensor_tensor(psum1[:, :], pair[:, 0:C], pair[:, C:2 * C], ALU.add).then_inc(m["psum1"], 1)

            def moe_out(f, b, t):
                m = moe[f]
                pool.wait_ge(m["combine"][t], HALF * b + 4)
                pool.wait_ge(m["psum1"], TILES * b + t + 1)
                pool.tensor_tensor(seq(DST[f], b, t * C, C), acc[:, (t % 2) * C:(t % 2 + 1) * C], psum1[:, :],
                                   ALU.add).then_inc(m["out"], 1)

            def att_x0_scale(b):
                pool.wait_ge(a["n2"], b + 1)
                pool.tensor_tensor(grp(t0[:, :], C), grp(n2[:, :], C),
                                   w0b[:, :].unsqueeze(1).to_broadcast([C, TILES, C]), ALU.mult).then_inc(a["x0_scaled"], 1)

            def att_x0(b):
                pool.wait_ge(a["x0_scaled"], b + 1)
                pool.tensor_tensor(grp(seq(X0, b), C), grp(t0[:, :], C),
                                   b0b[:, :].unsqueeze(1).to_broadcast([C, TILES, C]), ALU.add).then_inc(a["X0"], 1)

            def att_e2v(b):
                pool.wait_ge(a["e12"], b + 1)
                pool.tensor_tensor(e12[:, TOK:2 * TOK], e12[:, 2 * TOK:3 * TOK], vS[:, :], ALU.mult).then_inc(a["e2v"], 1)

            def att_xs(b):
                pool.tensor_tensor(xs[:, :], seq(X1, b), XR[:, :], ALU.add).then_inc(a["xs"], 1)

            pool.memset(bexp[:, :], 0.0).then_inc(s_z, 1)
            pool.memset(mhalf[:, :], -0.5).then_inc(s_const, 1)
            pool.memset(ones[:, :], 1.0).then_inc(s_const, 1)
            pool.wait_ge(s_const, 2)
            pool.sem_inc(a["shift"], 1)
            moe_var(0, 0)
            moe_rstd(0, 0)
            moe_shift(0, 0)
            moe_var(0, 1)
            moe_rstd(0, 1)
            moe_shift(0, 1)
            moe_var(0, 2)
            moe_rstd(0, 2)
            pool.wait_ge(s_vec, 48)
            pool.wait_ge(s_wa, 48)
            mix_weights()
            moe_pair(0, 0, 0)
            moe_shift(0, 2)
            moe_var(0, 3)
            moe_psum1(0, 0, 0)
            moe_rstd(0, 3)
            moe_pair(0, 0, 1)
            moe_out(0, 0, 0)
            moe_psum1(0, 0, 1)
            moe_pair(0, 0, 2)
            moe_out(0, 0, 1)
            moe_psum1(0, 0, 2)
            moe_pair(0, 0, 3)
            moe_out(0, 0, 2)
            moe_shift(0, 3)
            moe_psum1(0, 0, 3)
            moe_out(0, 0, 3)
            with pool.Fori(1, BATCHES - 1) as b:
                moe_pair(0, b, 0)
                moe_psum1(0, b, 0)
                att_var(b - 1)
                att_rstd(b - 1)
                moe_out(0, b, 0)
                moe_pair(0, b, 1)
                moe_psum1(0, b, 1)
                att_shift(b - 1)
                moe_pair(0, b, 2)
                moe_out(0, b, 1)
                moe_psum1(0, b, 2)
                moe_pair(0, b, 3)
                moe_out(0, b, 2)
                moe_psum1(0, b, 3)
                moe_out(0, b, 3)
            pool.wait_ge(s_vec, 48)
            att_x0_scale(0)
            att_x0(0)
            moe_pair(0, 3, 0)
            moe_psum1(0, 3, 0)
            att_var2(0)
            att_rstd2(0)
            att_shift2(0)
            moe_out(0, 3, 0)
            att_x0_scale(1)
            att_x0(1)
            moe_pair(0, 3, 1)
            moe_psum1(0, 3, 1)
            att_var(2)
            moe_out(0, 3, 1)
            moe_pair(0, 3, 2)
            moe_psum1(0, 3, 2)
            att_var2(1)
            moe_pair(0, 3, 3)
            att_rstd(2)
            att_rstd2(1)
            moe_out(0, 3, 2)
            att_shift2(1)
            moe_psum1(0, 3, 3)
            att_e2v(0)
            moe_out(0, 3, 3)
            att_shift(2)
            att_var(3)
            att_rstd(3)
            att_shift(3)
            with pool.Fori(1, BATCHES - 1) as b:
                att_var3(b - 1)
                att_rstd3(b - 1)
                att_shift3(b - 1)
                att_x0_scale(b + 1)
                att_x0(b + 1)
                att_xs(b - 1)
                att_var2(b + 1)
                att_rstd2(b + 1)
                att_shift2(b + 1)
                att_e2v(b)
                moe_var(1, b - 1)
                moe_rstd(1, b - 1)
                moe_shift(1, b - 1)
            att_var3(2)
            att_rstd3(2)
            att_shift3(2)
            att_xs(2)
            att_e2v(3)
            att_var3(3)
            att_rstd3(3)
            att_shift3(3)
            moe_pair(1, 0, 0)
            moe_psum1(1, 0, 0)
            moe_out(1, 0, 0)
            moe_pair(1, 0, 1)
            moe_psum1(1, 0, 1)
            moe_pair(1, 0, 2)
            moe_out(1, 0, 1)
            moe_var(1, 2)
            moe_rstd(1, 2)
            moe_shift(1, 2)
            moe_psum1(1, 0, 2)
            moe_pair(1, 0, 3)
            moe_out(1, 0, 2)
            moe_psum1(1, 0, 3)
            att_xs(3)
            moe_out(1, 0, 3)
            moe_var(1, 3)
            moe_rstd(1, 3)
            moe_shift(1, 3)
            with pool.Fori(1, BATCHES - 1) as b:
                moe_pair(1, b, 0)
                moe_psum1(1, b, 0)
                moe_out(1, b, 0)
                moe_pair(1, b, 1)
                moe_psum1(1, b, 1)
                moe_out(1, b, 1)
                moe_pair(1, b, 2)
                moe_psum1(1, b, 2)
                moe_out(1, b, 2)
                moe_pair(1, b, 3)
                moe_psum1(1, b, 3)
                moe_out(1, b, 3)
            moe_pair(1, 3, 0)
            moe_psum1(1, 3, 0)
            moe_out(1, 3, 0)
            moe_pair(1, 3, 1)
            moe_psum1(1, 3, 1)
            moe_out(1, 3, 1)
            moe_pair(1, 3, 2)
            moe_psum1(1, 3, 2)
            moe_pair(1, 3, 3)
            moe_out(1, 3, 2)
            moe_psum1(1, 3, 3)
            moe_out(1, 3, 3)


def kernel(**inputs):
    import numpy as np
    import concourse.bacc as bacc
    from concourse.bass_utils import run_bass_kernel_spmd

    g = {k.replace("L0_attn_", "").replace("L0_ffn_", ""): np.asarray(v) for k, v in inputs.items()}
    cc = np.ascontiguousarray
    vectors = [g[n] for n in ("time_decay", "time_first", "tmk", "tmv", "tmr", "ln1_w", "ln1_b", "ln2_w", "ln2_b",
                              "cmk", "cmr")]
    arrays = {
        "x_in": cc(g["x"].reshape(BATCHES * TOK, C)),
        "vectors": cc(np.stack(vectors, axis=1)),
        "ln0_w": cc(g["ln0_w"]), "ln0_b": cc(g["ln0_b"]),
        "w_att": cc(np.concatenate([g[n].T for n in ("Wk", "Wv", "Wr", "Wo", "Wfr")], axis=1)),
        "w_ffn_k": cc(g["Wfk"].T),
        "w_ffn_v": cc(g["Wfv"].T.reshape(HC, C, C).transpose(1, 0, 2).reshape(C, HC * C)),
        "w_exp": cc(g["We"].transpose(1, 0, 2).reshape(C, E * C)),
        "b_exp": cc(g["be"]),
        "w_gate": cc(g["Wg"]),
        "b_gate": cc(np.broadcast_to(g["bg"], (C, TILES, E)).reshape(C, TILES * E)),
        "ident": np.eye(C, dtype=np.float32),
    }
    nc = bacc.Bacc("TRN2", target_bir_lowering=False, num_devices=1)
    args = [nc.dram_tensor(f"in_{n}", v.shape, mybir.dt.from_np(v.dtype), kind="ExternalInput").ap()
            for n, v in arrays.items()]
    out = nc.dram_tensor("y_out", (BATCHES * TOK, C), F32, kind="ExternalOutput").ap()
    macaron_kernel(nc, *args, out)
    r = run_bass_kernel_spmd(nc, [{f"in_{n}": v for n, v in arrays.items()}], core_ids=[0])
    return r.results[0]["y_out"].reshape(BATCHES, TOK, C)
```
